# Optimizing a Trainium2 kernel written in Bass

```python
import numpy as np
import jax
import jax.numpy as jnp

def _softmax(x, axis=-1):
    return jax.nn.softmax(x, axis=axis)

def _gelu(x):
    return jax.nn.gelu(x, approximate=True)

def _silu(x):
    return jax.nn.silu(x)

def _sigmoid(x):
    return jax.nn.sigmoid(x)

def _layernorm(x, axis=-1, eps=1e-05):
    m = jnp.mean(x, axis=axis, keepdims=True)
    v = jnp.var(x, axis=axis, keepdims=True)
    return (x - m) / jnp.sqrt(v + eps)

def _scatter_add(tgt, idx, src, axis=0):
    return tgt.at[idx].add(src)

def _segment_sum(src, seg, n):
    return jax.ops.segment_sum(src, seg, n)
kernel_name = 'mk_decoder_postln_d1_seqx_r8_79df36'

def setup_inputs(seed: int=0):
    np.random.seed(seed)
    _w = jnp.asarray

    def _rec_inputs():
        import jax
        import jax.numpy as jnp
        _rk = jax.random.key(seed)
        x = -0.000929 + 1 * jax.random.normal(jax.random.fold_in(_rk, 1), (1, 1024, 128), jnp.float32)
        _lenS = 1024 - jax.random.randint(jax.random.fold_in(_rk, 7), (1,), 0, max(1, 1024 // 4) + 1, jnp.int32)
        _lenS2 = 6404 - jax.random.randint(jax.random.fold_in(_rk, 8), (1,), 0, max(1, 6404 // 4) + 1, jnp.int32)
        _ctx_1024P = jax.random.normal(jax.random.fold_in(_rk, 11), (1, 16, 128), jnp.float32)
        _ctx_1024c = jax.random.dirichlet(jax.random.fold_in(_rk, 511), 0.3 * jnp.ones((16,), jnp.float32), (1, 6404))
        _ctx_1024t = jnp.einsum('bsk,bkd->bsd', _ctx_1024c, _ctx_1024P)
        _ctx_1024t = _ctx_1024t * jax.lax.rsqrt(jnp.mean(jnp.square(_ctx_1024t)) + 1e-12) * 0.953939
        ctx_1024 = -1.52775e-05 + 0.999936 * (_ctx_1024t + 0.3 * jax.random.normal(jax.random.fold_in(_rk, 611), (1, 6404, 128), jnp.float32))
        return (x, ctx_1024)
    x, ctx_1024 = _rec_inputs()

    def _L0_attn_setup():
        import jax, jax.numpy as jnp
        import numpy as np
        B, L, D = (2, 1024, 128)
        FILTER_ORDER = 64
        FILTER_HIDDEN = 64

        def positional_embedding(seq_len, emb_dim):
            positions = jnp.arange(seq_len, dtype=jnp.float32)[:, None]
            div_term = jnp.exp(jnp.arange(0, emb_dim, 2, dtype=jnp.float32) * -(jnp.log(10000.0) / emb_dim))
            pe = jnp.zeros((seq_len, emb_dim), jnp.float32)
            pe = pe.at[:, 0::2].set(jnp.sin(positions * div_term))
            pe = pe.at[:, 1::2].set(jnp.cos(positions * div_term))
            return pe

        def causal_fft_conv(v, h):
            seq_len = v.shape[1]
            n = 2 * seq_len
            v_f = jnp.fft.rfft(v, n=n, axis=1)
            h_f = jnp.fft.rfft(h, n=n, axis=0)[None]
            y = jnp.fft.irfft(v_f * h_f, n=n, axis=1)[:, :seq_len, :]
            return y.astype(v.dtype)
        key = jax.random.key(seed)
        ks = jax.random.split(key, 12)
        s = lambda fan_in: 1.0 / np.sqrt(fan_in)
        return {'x': jax.random.normal(ks[0], (B, L, D), dtype=jnp.float32), 'Wu': jax.random.normal(ks[1], (D, D), dtype=jnp.float32) * s(D), 'bu': jnp.zeros((D,), jnp.float32), 'Wv': jax.random.normal(ks[2], (D, D), dtype=jnp.float32) * s(D), 'bv': jnp.zeros((D,), jnp.float32), 'W1': jax.random.normal(ks[3], (FILTER_ORDER, FILTER_HIDDEN), dtype=jnp.float32) * s(FILTER_ORDER), 'b1': jnp.zeros((FILTER_HIDDEN,), jnp.float32), 'W2': jax.random.normal(ks[4], (FILTER_HIDDEN, FILTER_HIDDEN), dtype=jnp.float32) * s(FILTER_HIDDEN), 'b2': jnp.zeros((FILTER_HIDDEN,), jnp.float32), 'W3': jax.random.normal(ks[5], (FILTER_HIDDEN, D), dtype=jnp.float32) * s(FILTER_HIDDEN), 'b3': jnp.zeros((D,), jnp.float32), 'Wo': jax.random.normal(ks[6], (D, D), dtype=jnp.float32) * s(D), 'bo': jnp.zeros((D,), jnp.float32)}
    _L0_attn_all = _L0_attn_setup()
    _L0_attn_in = {k: v for k, v in _L0_attn_all.items() if k in ('Wu', 'bu', 'Wv', 'bv', 'W1', 'b1', 'W2', 'b2', 'W3', 'b3', 'Wo', 'bo')}
    del _L0_attn_all

    def _L0_xattn_setup():
        import jax, jax.numpy as jnp
        import numpy as np
        DIM = 128
        H = 16
        D = 64
        INNER = H * D
        EPS = 1e-05

        def layernorm(x, w, b):
            mu = jnp.mean(x, axis=-1, keepdims=True)
            var = jnp.var(x, axis=-1, keepdims=True)
            return (x - mu) * jax.lax.rsqrt(var + EPS) * w + b
        key = jax.random.key(seed)
        ks = jax.random.split(key, 8)
        B, N, S = (4, 32, 1024)
        s = 1.0 / np.sqrt(DIM)
        return {'latents': jax.random.normal(ks[0], (B, N, DIM), jnp.float32), 'context': jax.random.normal(ks[1], (B, S, DIM), jnp.float32), 'ln_l_w': jnp.ones((DIM,), jnp.float32), 'ln_l_b': jnp.zeros((DIM,), jnp.float32), 'ln_c_w': jnp.ones((DIM,), jnp.float32), 'ln_c_b': jnp.zeros((DIM,), jnp.float32), 'Wq': jax.random.normal(ks[2], (DIM, INNER), jnp.float32) * s, 'Wkv': jax.random.normal(ks[3], (DIM, 2 * INNER), jnp.float32) * s, 'Wo': jax.random.normal(ks[4], (INNER, DIM), jnp.float32) * (1.0 / np.sqrt(INNER)), 'bo': jnp.zeros((DIM,), jnp.float32)}
    _L0_xattn_all = _L0_xattn_setup()
    _L0_xattn_in = {k: v for k, v in _L0_xattn_all.items() if k in ('ln_l_w', 'ln_l_b', 'ln_c_w', 'ln_c_b', 'Wq', 'Wkv', 'Wo', 'bo')}
    del _L0_xattn_all

    def _L0_ffn_setup():
        import jax, jax.numpy as jnp
        import numpy as np
        B, T, D, E, TOP_K = (4, 512, 128, 8, 2)
        CAPACITY_FACTOR = 1.5
        key = jax.random.key(seed)
        k1, k2, k3 = jax.random.split(key, 3)
        x = jax.random.normal(k1, (B, T, D), dtype=jnp.float32)
        Wr = jax.random.normal(k2, (E, D), dtype=jnp.float32) * 0.02
        We = jax.random.normal(k3, (E, D, D), dtype=jnp.float32) * 0.02
        return {'x': x, 'Wr': Wr, 'We': We}
    _L0_ffn_all = _L0_ffn_setup()
    _L0_ffn_in = {k: v for k, v in _L0_ffn_all.items() if k in ('Wr', 'We')}
    del _L0_ffn_all
    return {'x': x, 'ctx_1024': ctx_1024, 'L0_attn_Wu': _L0_attn_in['Wu'], 'L0_attn_bu': _L0_attn_in['bu'], 'L0_attn_Wv': _L0_attn_in['Wv'], 'L0_attn_bv': _L0_attn_in['bv'], 'L0_attn_W1': _L0_attn_in['W1'], 'L0_attn_b1': _L0_attn_in['b1'], 'L0_attn_W2': _L0_attn_in['W2'], 'L0_attn_b2': _L0_attn_in['b2'], 'L0_attn_W3': _L0_attn_in['W3'], 'L0_attn_b3': _L0_attn_in['b3'], 'L0_attn_Wo': _L0_attn_in['Wo'], 'L0_attn_bo': _L0_attn_in['bo'], 'L0_xattn_ln_l_w': _L0_xattn_in['ln_l_w'], 'L0_xattn_ln_l_b': _L0_xattn_in['ln_l_b'], 'L0_xattn_ln_c_w': _L0_xattn_in['ln_c_w'], 'L0_xattn_ln_c_b': _L0_xattn_in['ln_c_b'], 'L0_xattn_Wq': _L0_xattn_in['Wq'], 'L0_xattn_Wkv': _L0_xattn_in['Wkv'], 'L0_xattn_Wo': _L0_xattn_in['Wo'], 'L0_xattn_bo': _L0_xattn_in['bo'], 'L0_ffn_Wr': _L0_ffn_in['Wr'], 'L0_ffn_We': _L0_ffn_in['We']}

def reference(x, ctx_1024, L0_attn_Wu, L0_attn_bu, L0_attn_Wv, L0_attn_bv, L0_attn_W1, L0_attn_b1, L0_attn_W2, L0_attn_b2, L0_attn_W3, L0_attn_b3, L0_attn_Wo, L0_attn_bo, L0_xattn_ln_l_w, L0_xattn_ln_l_b, L0_xattn_ln_c_w, L0_xattn_ln_c_b, L0_xattn_Wq, L0_xattn_Wkv, L0_xattn_Wo, L0_xattn_bo, L0_ffn_Wr, L0_ffn_We):
    import jax
    import jax.numpy as jnp

    def _L0_attn_ref(x, Wu, bu, Wv, bv, W1, b1, W2, b2, W3, b3, Wo, bo):
        import jax, jax.numpy as jnp
        import numpy as np
        B, L, D = (2, 1024, 128)
        FILTER_ORDER = 64
        FILTER_HIDDEN = 64

        def positional_embedding(seq_len, emb_dim):
            positions = jnp.arange(seq_len, dtype=jnp.float32)[:, None]
            div_term = jnp.exp(jnp.arange(0, emb_dim, 2, dtype=jnp.float32) * -(jnp.log(10000.0) / emb_dim))
            pe = jnp.zeros((seq_len, emb_dim), jnp.float32)
            pe = pe.at[:, 0::2].set(jnp.sin(positions * div_term))
            pe = pe.at[:, 1::2].set(jnp.cos(positions * div_term))
            return pe

        def causal_fft_conv(v, h):
            seq_len = v.shape[1]
            n = 2 * seq_len
            v_f = jnp.fft.rfft(v, n=n, axis=1)
            h_f = jnp.fft.rfft(h, n=n, axis=0)[None]
            y = jnp.fft.irfft(v_f * h_f, n=n, axis=1)[:, :seq_len, :]
            return y.astype(v.dtype)
        seq_len = x.shape[1]
        u = x @ Wu + bu
        v = x @ Wv + bv
        pos_emb = positional_embedding(seq_len, FILTER_ORDER)
        h = jax.nn.gelu(pos_emb @ W1 + b1)
        h = jax.nn.gelu(h @ W2 + b2)
        h = h @ W3 + b3
        t = jnp.arange(seq_len, dtype=jnp.float32)
        decay = jnp.exp(-0.01 * t)[:, None]
        h = h * decay
        v_conv = causal_fft_conv(v, h)
        y = u * v_conv
        y = y @ Wo + bo
        return y

    def _L0_xattn_ref(latents, context, ln_l_w, ln_l_b, ln_c_w, ln_c_b, Wq, Wkv, Wo, bo):
        import jax, jax.numpy as jnp
        import numpy as np
        DIM = 128
        H = 16
        D = 64
        INNER = H * D
        EPS = 1e-05

        def layernorm(x, w, b):
            mu = jnp.mean(x, axis=-1, keepdims=True)
            var = jnp.var(x, axis=-1, keepdims=True)
            return (x - mu) * jax.lax.rsqrt(var + EPS) * w + b
        b, n, _ = latents.shape
        s = context.shape[1]
        lat = layernorm(latents, ln_l_w, ln_l_b)
        ctx = layernorm(context, ln_c_w, ln_c_b)
        q = (lat @ Wq).reshape(b, n, H, D).transpose(0, 2, 1, 3)
        kv = ctx @ Wkv
        k, v = jnp.split(kv, 2, axis=-1)
        k = k.reshape(b, s, H, D).transpose(0, 2, 1, 3)
        v = v.reshape(b, s, H, D).transpose(0, 2, 1, 3)
        scale = D ** (-0.5)
        attn = jnp.einsum('bhnd,bhsd->bhns', q, k) * scale
        attn = jnp.clip(attn, -11.0, 11.0)
        attn = jax.nn.softmax(attn, axis=-1)
        out = jnp.einsum('bhns,bhsd->bhnd', attn, v)
        out = out.transpose(0, 2, 1, 3).reshape(b, n, INNER)
        return out @ Wo + bo

    def _L0_ffn_ref(x, Wr, We):
        import jax, jax.numpy as jnp
        import numpy as np
        B, T, D, E, TOP_K = (4, 512, 128, 8, 2)
        CAPACITY_FACTOR = 1.5
        Bb, Tt, Dd = x.shape
        Ee = Wr.shape[0]
        K = TOP_K
        C = int(Tt * K / Ee * CAPACITY_FACTOR) + 1
        logits = jnp.einsum('btd,ed->bte', x, Wr)
        top_vals, top_idx = jax.lax.top_k(logits, K)
        w = jax.nn.softmax(top_vals, axis=-1)
        flat_e = top_idx.reshape(Bb, Tt * K)
        oh = jax.nn.one_hot(flat_e, Ee, dtype=jnp.int32)
        pos_all = jnp.cumsum(oh, axis=1) - oh
        pos = jnp.take_along_axis(pos_all, flat_e[..., None], axis=-1)[..., 0]
        keep = pos < C
        b_idx = jnp.arange(Bb, dtype=jnp.int32)[:, None]
        dst = (b_idx * Ee + flat_e) * C + pos
        dst = jnp.where(keep, dst, Bb * Ee * C).reshape(-1)
        x_rep = jnp.repeat(x, K, axis=1).reshape(-1, Dd)
        buf = jnp.zeros((Bb * Ee * C, Dd), dtype=x.dtype).at[dst].add(x_rep, mode='drop')
        expert_in = buf.reshape(Bb, Ee, C, Dd)
        expert_out = jnp.einsum('becd,edf->becf', expert_in, We)
        gathered = jnp.take(expert_out.reshape(Bb * Ee * C, Dd), dst, axis=0, mode='fill', fill_value=0.0)
        gathered = gathered.reshape(Bb, Tt, K, Dd)
        out = jnp.einsum('btk,btkd->btd', w, gathered)
        return out
    x = _layernorm(x + _L0_attn_ref(x, L0_attn_Wu, L0_attn_bu, L0_attn_Wv, L0_attn_bv, L0_attn_W1, L0_attn_b1, L0_attn_W2, L0_attn_b2, L0_attn_W3, L0_attn_b3, L0_attn_Wo, L0_attn_bo), axis=-1)
    x = _layernorm(x + _L0_xattn_ref(x, ctx_1024, L0_xattn_ln_l_w, L0_xattn_ln_l_b, L0_xattn_ln_c_w, L0_xattn_ln_c_b, L0_xattn_Wq, L0_xattn_Wkv, L0_xattn_Wo, L0_xattn_bo), axis=-1)
    x = _layernorm(x + _L0_ffn_ref(x, L0_ffn_Wr, L0_ffn_We), axis=-1)
    return x

_drawn_inputs = setup_inputs


def setup_inputs(seed=0):
    import zlib

    import numpy as np

    out = dict(_drawn_inputs(seed))
    spreads = {'L0_attn_bu': (0.0, 0.1),
     'L0_attn_bv': (0.0, 0.1),
     'L0_attn_b1': (0.0, 0.1),
     'L0_attn_b2': (0.0, 0.1),
     'L0_attn_b3': (0.0, 0.1),
     'L0_attn_bo': (0.0, 0.1),
     'L0_xattn_ln_l_w': (1.0, 0.2),
     'L0_xattn_ln_l_b': (0.0, 0.307),
     'L0_xattn_ln_c_w': (1.0, 0.2),
     'L0_xattn_ln_c_b': (0.0, 0.1),
     'L0_xattn_bo': (0.0, 0.1)}
    factors = {}
    for name, (base, spread) in spreads.items():
        noise = np.random.default_rng([zlib.crc32(name.encode()), seed]).standard_normal(out[name].shape)
        drawn = base * np.exp(spread * noise) if base else spread * noise
        out[name] = jnp.asarray(drawn.astype(out[name].dtype))
    for name, factor in factors.items():
        out[name] = (out[name] * factor).astype(out[name].dtype)
    return out
```

```python
from contextlib import ExitStack

import numpy as np

import concourse.bass as bass
from concourse import mybir

F32 = mybir.dt.float32
F32R = mybir.dt.float32r
U32 = mybir.dt.uint32
ALU = mybir.AluOpType
ACT = mybir.ActivationFunctionType

P = 128
D = 128
L = 1024
LT = L // P
NH = 2
HALF = L // NH
S = 6404
ST = S // P
SR = S - ST * P
TILES = ST + 1
H = 16
DH = 64
PAIRS = H // 2
CT = 4
CK = CT * P
WHOLE = ST // CT
TAIL_TILES = TILES - WHOLE * CT
TAIL_K = S - WHOLE * CK
GC = 10
E = 8
CAP = int(L * 2 / E * 1.5) + 1
FO = 64
BLK = 256
NB = L // BLK
W = 2 * BLK
CLIP = 11.0
EPS = 1e-5
SCALE = DH ** -0.5
ROUNDS = WHOLE + 1 + 2
LAG = 2
PREV_SLOTS = 3


def constants():
    ident = np.eye(P)
    earlier = np.triu(np.ones((P, P)), 1)
    expert = np.tile(np.arange(E), (P, LT))
    t = np.arange(L)
    decay = np.exp(np.float32(-0.01) * t.astype(np.float32)).reshape(LT, P).T
    pack = np.concatenate([ident, earlier, expert, decay], 1).astype(np.float32)

    div = np.exp(np.arange(0, FO, 2, dtype=np.float32) * np.float32(-(np.log(10000.0) / FO)))
    ang = t.astype(np.float32)[:, None] * div.astype(np.float32)
    pe = np.zeros((L, FO), np.float32)
    pe[:, 0::2], pe[:, 1::2] = np.sin(ang), np.cos(ang)

    n, k = np.arange(W)[:, None], np.arange(BLK)[None, :]
    cos, sin = np.cos(2 * np.pi * n * k / W), np.sin(2 * np.pi * n * k / W)
    nyquist = np.cos(np.pi * n)
    cos_n, sin_n = cos[:, :P].copy(), sin[:, :P].copy()
    cos_n[:, :1], sin_n[:, :1] = nyquist, nyquist
    forward = np.concatenate([cos, sin, cos_n, sin_n], 1)
    inv_cos = 2 * cos[BLK:].T / W
    inv_cos[0] /= 2
    inv_sin = 2 * sin[BLK:].T / W
    inv_sin[0] = nyquist[BLK:, 0] / W
    inverse = np.concatenate([inv_cos, inv_sin], 0)
    return {"c_pack": pack, "c_pe": np.ascontiguousarray(pe.T),
            "c_fwd": forward.astype(np.float32), "c_inv": inverse.astype(np.float32)}


def build(nc, a, out, pairs=PAIRS, probe=None):
    ctx = ExitStack()
    with ctx:
        def sb(name, shape, dt=F32):
            return ctx.enter_context(nc.sbuf_tensor(name, shape, dt))

        def sem(name):
            return ctx.enter_context(nc.semaphore(name))

        pack = sb("pack", [P, 2 * P + LT * E + LT])
        ident, earlier = pack[:, 0:P], pack[:, P:2 * P]
        expert_no = pack[:, 2 * P:2 * P + LT * E].rearrange("p (j e) -> p j e", e=E)
        decay = pack[:, 2 * P + LT * E:]
        ones = sb("ones", [P, P])
        pe_t = sb("pe_t", [FO, L])
        fwd = sb("fwd", [P, W // P, 6 * P])
        inv = sb("inv", [P, W // P, BLK])
        x_sb = sb("x_sb", [P, LT, D])
        bias_rows = sb("bias_rows", [1, 4, D])
        b_v, b_h, b_o, b_x = (bias_rows[0:1, i, :] for i in range(4))
        cols = sb("cols", [P, 8])
        w_uv = sb("w_uv", [P, 2, D])
        w_12 = sb("w_12", [FO, 2, FO])
        w_3 = sb("w_3", [FO, D])
        w_o = sb("w_o", [P, D])
        w_router = sb("w_router", [P, E])
        w_experts = sb("w_experts", [P, E, D])
        w_xo = sb("w_xo", [P, PAIRS, D])
        w_kv = sb("w_kv", [P, 2, P])
        w_q = sb("w_q", [P, 2, 2, DH])

        keys_t = sb("keys_t", [P, S])
        stage = sb("stage", [P, 2, CK])
        k_parts = sb("k_parts", [P, 2, 2, CK], F32R)
        k_tail = sb("k_tail", [P, 2, TAIL_TILES * P], F32R)
        v_tail = sb("v_tail", [P, TAIL_TILES, P])
        q_parts = sb("q_parts", [P, 2, 2, L], F32R)
        lat_t = sb("lat_t", [P, L])
        probs = sb("probs", [P, CT, NH, 2, HALF])
        heads_t = sb("heads_t", [P, PAIRS, L])
        x1 = sb("x1", [P, LT, D])
        scratch = sb("scratch", [P, 8])
        small = sb("small", [P, 5 * LT * E])

        keys_raw = sb("keys_raw", [P, ST, D])

        def carve(t, at, shape):
            n = int(np.prod(shape[1:]))
            view = t[0:shape[0], at:at + n]
            if len(shape) == 3:
                view = view.rearrange("p (a b) -> p a b", b=shape[2])
            if len(shape) == 4:
                view = view.rearrange("p (a b c) -> p a b c", b=shape[2], c=shape[3])
            return view

        flat = probs[:, :, :, :, :].rearrange("p a b c d -> p (a b c d)")
        keys_last = sb("keys_last", [SR, D])
        raw_flat = keys_raw[:, :, :].rearrange("p a b -> p (a b)")
        sums = carve(raw_flat, 2 * L, [P, NH, 2, HALF])
        recip = carve(raw_flat, 4 * L, [P, NH, HALF])
        v_sb = carve(raw_flat, 5 * L, [P, 2, CT, P])
        heads_flat = heads_t[:, :, :].rearrange("p a b -> p (a b)")
        x_t = carve(heads_flat, 0, [P, L])
        h1_t = carve(heads_flat, L, [FO, L])
        h2_t = carve(heads_flat, 2 * L, [FO, L])
        h_sb = carve(heads_flat, 3 * L, [P, LT, D])
        v_time = carve(heads_flat, 4 * L, [P, LT, D])
        u_t = carve(heads_flat, 5 * L, [P, L])
        y_t = carve(heads_flat, 6 * L, [P, L])
        resid = carve(heads_flat, 7 * L, [P, LT, D])
        v_cos = carve(flat, 0, [P, 2, NB, D])
        v_sin = carve(flat, L, [P, 2, NB, D])
        h_cos = carve(flat, 2 * L, [P, 2, NB, D])
        h_sin = carve(flat, 3 * L, [P, 2, NB, D])
        h_cos_n = carve(flat, 4 * L, [P, 2, NB, D])
        y_cos = carve(flat, 5 * L, [P, 2, NB, D])
        y_sin = carve(flat, 6 * L, [P, 2, NB, D])
        product_a = carve(flat, 7 * L, [P, 2, NB, D])
        product_b = carve(raw_flat, 0, [P, 2, NB, D])

        key_stat = sb("key_stat", [P, TILES, 6])
        key_mv = sb("key_mv", [P, TILES, 2])
        key_rstd = sb("key_rstd", [P, TILES])
        half_neg = sb("half_neg", [P, TILES])
        row_stat = sb("row_stat", [P, LT, 6])
        row_mv = sb("row_mv", [P, LT, 2])
        row_rstd = sb("row_rstd", [P, LT])
        bu_col, b1_col, b2_col, lw_col, lb_col, cw_col, cb_col = (cols[:, i:i + 1] for i in range(7))

        lat = keys_raw[:, 8:16, :]
        x2 = carve(flat, 0, [P, LT, D])
        x2_t = carve(flat, L, [P, L])
        x3 = carve(flat, 2 * L, [P, LT, D])
        moe = carve(flat, 3 * L, [P, LT, D])
        gate_one, gate_two, kept, chosen = (small[:, i * LT * E:(i + 1) * LT * E].rearrange("p (j e) -> p j e", e=E)
                                            for i in (0, 1, 2, 4))
        chosen_pad = small[:, 3 * LT * E:5 * LT * E]
        logits = sb("logits", [P, LT, E])
        top = sb("top", [P, LT, E])
        top_at = sb("top_at", [P, LT, E], U32)
        top_no = sb("top_no", [P, LT, E])
        weight = sb("weight", [P, 4, LT])

        scores = ctx.enter_context(nc.psum_tensor("scores", [P, NH, 2, HALF], F32))
        acc = ctx.enter_context(nc.psum_tensor("acc", [P, NH, HALF], F32))
        proj = ctx.enter_context(nc.psum_tensor("proj", [P, 2, HALF], F32))
        sc0 = scores[:, 0, :, :].rearrange("p b n -> p (b n)")
        sc1 = scores[:, 1, :, :].rearrange("p b n -> p (b n)")
        pj = proj[:, :, :].rearrange("p b n -> p (b n)")
        ac = acc[:, :, :].rearrange("p b n -> p (b n)")

        def tiles(view):
            return view.rearrange("p (j d) -> p j d", d=D)

        x_in, pack_in, conv_w_in, dft_in, late_in = (sem(n) for n in
                                                     ("x_in", "pack_in", "conv_w_in", "dft_in", "late_in"))
        key_in = [sem(f"key_in{g}") for g in range(ST // GC)]
        last_key_in = sem("last_key_in")
        ones_set = sem("ones_set")
        pad_set = sem("pad_set")
        key_stats, key_rstds, keys_normed = sem("key_stats"), sem("key_rstds"), sem("keys_normed")
        keys_turned, keys_copied = sem("keys_turned"), sem("keys_copied")
        pe_step, act_step, dve_step = sem("pe_step"), sem("act_step"), sem("dve_step")
        dve_link, pool_link = sem("dve_link"), sem("pool_link")
        row_stats, row_rstds = sem("row_stats"), sem("row_rstds")
        weights_in = sem("weights_in")
        stage_in = [sem("stage_in0"), sem("stage_in1")]
        proj_ready, act_round, dve_round = sem("proj_ready"), sem("act_round"), sem("dve_round")
        den_ready, den_read, heads_done = sem("den_ready"), sem("den_read"), sem("heads_done")
        scores_ready, exp_done, clip_done = sem("scores_ready"), sem("exp_done"), sem("clip_done")
        sum_done, pv_done = sem("sum_done"), sem("pv_done")
        tail_pe, tail_act, tail_dve = sem("tail_pe"), sem("tail_act"), sem("tail_dve")
        moe_ready, moe_added = sem("moe_ready"), sem("moe_added")
        stored = sem("stored")

        PE_STEPS = ["x_t", "h1", "v", "h2", "u", "h3", "v_dft0", "v_dft1", "v_dft2", "v_dft3",
                    "h_dft0", "h_dft1", "h_dft2", "h_dft3", "h_dft4", "conv", "attn", "lat_t"]
        ACT_STEPS = ["x_t", "h1", "v", "h2", "u", "v_dft0", "v_dft1", "v_dft2", "v_dft3",
                     "h_dft0", "h_dft1", "h_dft2", "h_dft3", "h_dft4", "lat_t"]
        DVE_STEPS = ["h", "spectrum", "y", "resid", "lat"]

        def pe_did(name):
            return PE_STEPS.index(name) + 1

        def act_did(name):
            return ACT_STEPS.index(name) + 1

        def dve_did(name):
            return DVE_STEPS.index(name) + 1

        def kv_round(p, c):
            return p * ROUNDS + c + 3

        block = ctx.enter_context(nc.Block())

        @block.sync
        def _(sp):
            sp.dma_start(x_sb[:, :, :], a["x"].rearrange("b (j p) d -> p (b j) d", p=P)).then_inc(x_in, 16)
            sp.dma_start(pack[:, :], a["c_pack"]).then_inc(pack_in, 16)
            keys = a["ctx_1024"][0, 0:ST * P, :].rearrange("(p j) d -> p j d", j=ST)
            for g in range(ST // GC):
                sp.dma_start(keys_raw[:, g * GC:(g + 1) * GC, :], keys[:, g * GC:(g + 1) * GC, :])\
                    .then_inc(key_in[g], 16)
            sp.dma_start(keys_last[:, :], a["ctx_1024"][0, ST * P:S, :]).then_inc(last_key_in, 16)

            wkv = a["L0_xattn_Wkv"].rearrange("d (two n) -> d two n", two=2)

            def load_weights(p):
                sp.dma_start(w_kv[:, :, :], wkv[:, :, bass.ds(p * P, P)]).then_inc(weights_in, 16)
                for copy in range(2):
                    wq = a["L0_xattn_Wq"][:, bass.ds(p * P, P)].rearrange("d (h n) -> d h n", h=2)
                    sp.dma_start(w_q[:, :, copy, :], wq).then_inc(weights_in, 16)

            load_weights(0)
            sp.dma_start(w_experts[:, :, :], a["L0_ffn_We"].rearrange("e d f -> d e f")).then_inc(late_in, 16)
            sp.dma_start(w_xo[:, :, :], a["L0_xattn_Wo"].rearrange("(g p) d -> p g d", p=P)).then_inc(late_in, 16)
            sp.dma_start(w_router[:, :], a["router_t"]).then_inc(late_in, 16)
            sp.wait_ge(keys_copied, WHOLE + 1)
            with sp.Fori(0, pairs) as p:
                with sp.Fori(0, (WHOLE - 2) // 2) as i:
                    for b in range(2):
                        sp.wait_ge(proj_ready, kv_round(p, i * 2 + b))
                        sp.dma_start(stage[:, b, :], keys_t[:, bass.ds(i * (2 * CK) + (b + 2) * CK, CK)])\
                            .then_inc(stage_in[b], 16)
                sp.wait_ge(proj_ready, kv_round(p, WHOLE))
                load_weights((p + 1) % pairs)
            sp.wait_ge(tail_dve, 5)
            sp.dma_start(out.rearrange("b (j p) d -> p (b j) d", p=P), moe).then_inc(stored, 16)
            sp.wait_ge(stored, 16)

        @block.gpsimd
        def _(pool):
            pool.memset(half_neg[:, :], -0.5)
            pool.memset(k_tail[:, :, :].bitcast(F32), 0.0).then_inc(pad_set, 1)
            links = 0

            def rstd(to, mv):
                nonlocal links
                pool.tensor_scalar(to, mv, EPS, None, ALU.add).then_inc(pool_link, 1)
                links += 1
                pool.wait_ge(pool_link, links)
                return pool.tensor_tensor(to, to, half_neg[0:to.shape[0], 0:to.shape[1]], ALU.pow)

            pool.wait_ge(pad_set, 1)
            for g in range(ST // GC):
                pool.wait_ge(key_stats, g + 1)
                span = slice(g * GC, (g + 1) * GC)
                rstd(key_rstd[:, span], key_mv[:, span, 1]).then_inc(key_rstds, 1)
            pool.wait_ge(key_stats, ST // GC + 1)
            rstd(key_rstd[0:SR, ST:TILES], key_mv[0:SR, ST:TILES, 1]).then_inc(key_rstds, 1)
            for n in range(4):
                pool.wait_ge(row_stats, n + 1)
                rstd(row_rstd[:, :], row_mv[:, :, 1]).then_inc(row_rstds, 1)

        @block.scalar
        def _(act):
            act.dma_start(pe_t[:, :], a["c_pe"]).then_inc(conv_w_in, 16)
            for i, n in enumerate(("L0_attn_W1", "L0_attn_W2")):
                act.dma_start(w_12[:, i, :], a[n]).then_inc(conv_w_in, 16)
            act.dma_start(w_3[:, :], a["L0_attn_W3"]).then_inc(conv_w_in, 16)
            for i, n in enumerate(("L0_attn_Wu", "L0_attn_Wv")):
                act.dma_start(w_uv[:, i, :], a[n]).then_inc(conv_w_in, 16)
            act.dma_start(w_o[:, :], a["L0_attn_Wo"]).then_inc(conv_w_in, 16)
            for i, n in enumerate(("L0_attn_bv", "L0_attn_b3", "L0_attn_bo", "L0_xattn_bo")):
                act.dma_start(bias_rows[0:1, i, :], a[n].rearrange("(o d) -> o d", o=1)).then_inc(conv_w_in, 16)
            for i, n in enumerate(("L0_attn_bu", "L0_attn_b1", "L0_attn_b2", "L0_xattn_ln_l_w",
                                   "L0_xattn_ln_l_b", "L0_xattn_ln_c_w", "L0_xattn_ln_c_b")):
                rows = a[n].shape[0]
                act.dma_start(cols[0:rows, i:i + 1], a[n].rearrange("(d o) -> d o", o=1)).then_inc(conv_w_in, 16)
            act.dma_start(fwd[:, :, :], a["c_fwd"].rearrange("(w p) k -> p w k", p=P)).then_inc(dft_in, 16)
            act.dma_start(inv[:, :, :], a["c_inv"].rearrange("(w p) k -> p w k", p=P)).then_inc(dft_in, 16)

            def copy(to, frm, step):
                act.wait_ge(pe_step, pe_did(step))
                nc.scalar.activation(to, frm, ACT.Copy).then_inc(act_step, 1)

            def turn_keys(k):
                n = CK if k < WHOLE else TAIL_K
                act.wait_ge(keys_turned, k + 1)
                nc.scalar.activation(keys_t[:, k * CK:k * CK + n], acc[:, k % 2, 0:n], ACT.Identity,
                                     bias=cb_col, scale=cw_col).then_inc(keys_copied, 1)

            copy(x_t, sc0, "x_t")
            act.wait_ge(conv_w_in, 18 * 16)
            act.wait_ge(pe_step, pe_did("h1"))
            nc.scalar.activation(h1_t, sc1[0:FO, :], ACT.Gelu_apprx_tanh, bias=b1_col[0:FO, :]).then_inc(act_step, 1)
            copy(v_time, tiles(sc0), "v")
            act.wait_ge(pe_step, pe_did("h2"))
            nc.scalar.activation(h2_t, pj[0:FO, :], ACT.Gelu_apprx_tanh, bias=b2_col[0:FO, :]).then_inc(act_step, 1)
            act.wait_ge(pe_step, pe_did("u"))
            nc.scalar.activation(u_t, pj, ACT.Identity, bias=bu_col).then_inc(act_step, 1)
            for k in range(4):
                turn_keys(k)
            for i, (to, f) in enumerate(((v_cos, 0), (v_cos, 1), (v_sin, 0), (v_sin, 1))):
                copy(to[:, f, :, :], scores[:, i // 2, i % 2, :].rearrange("p (b d) -> p b d", d=D), f"v_dft{i}")
            for i, (to, f) in enumerate(((h_cos, 0), (h_cos, 1), (h_sin, 0), (h_sin, 1), (h_cos_n, 0))):
                bank = proj[:, i, :] if i < 2 else scores[:, (i - 2) // 2, (i - 2) % 2, :]
                copy(to[:, f, :, :], bank.rearrange("p (b d) -> p b d", d=D), f"h_dft{i}")
            for k in range(4, WHOLE + 1):
                turn_keys(k)
            act.wait_ge(pe_step, pe_did("lat_t"))
            nc.scalar.activation(lat_t[:, :], sc1, ACT.Identity, bias=lb_col, scale=lw_col).then_inc(act_step, 1)

            for i in range(2):
                nc.scalar.activation(scratch[:, i:i + 1], cols[:, 0:1], ACT.Exp).then_inc(exp_done, 1)

            def kv_copies(n, buf, width, vt):
                act.wait_ge(proj_ready, n)
                dst = k_parts[:, buf, :, :] if buf < 2 else k_tail[:, :, :]
                for h in range(2):
                    r = slice(h * DH, (h + 1) * DH)
                    nc.scalar.activation(dst[r, h, 0:width], proj[r, 0, 0:width], ACT.Copy)
                if buf < 2:
                    nc.scalar.activation(v_sb[:, buf, :, :], proj[:, 1, :].rearrange("p (t n) -> p t n", n=P),
                                         ACT.Copy).then_inc(act_round, 1)
                else:
                    nc.scalar.activation(v_tail[:, 0:vt - 1, :],
                                         proj[:, 1, 0:(vt - 1) * P].rearrange("p (t n) -> p t n", n=P), ACT.Copy)
                    nc.scalar.activation(v_tail[0:SR, vt - 1, :], proj[0:SR, 1, (vt - 1) * P:vt * P],
                                         ACT.Copy).then_inc(act_round, 1)

            def q_copy(n, h):
                act.wait_ge(proj_ready, n)
                nc.scalar.activation(q_parts[:, h, 0, :], pj, ACT.Copy).then_inc(act_round, 1)

            def exps(T, slot, rows=P):
                act.wait_ge(pv_done, T + 1)
                act.wait_ge(sum_done, T + 1)
                for n in range(NH):
                    act.wait_ge(scores_ready, T * 2 + n + 1)
                    nc.scalar.activation(probs[0:rows, slot, n, :, :], scores[0:rows, n, :, :], ACT.Exp,
                                         scale=SCALE).then_inc(exp_done, 1)

            def chunk(p, T, n, width=CK, buf=0):
                exps(T, 0)
                exps(T + 1, 1)
                kv_copies(n, buf, width, TAIL_TILES)
                exps(T + 2, 2)
                exps(T + 3, 3)

            act.wait_ge(pad_set, 1)
            kv_copies(1, 0, CK, 0)
            q_copy(2, 0)
            q_copy(3, 1)
            with act.Fori(0, pairs) as p:
                chunk(p, p * TILES, kv_round(p, 1), buf=1)
                with act.Fori(0, (WHOLE - 2) // 2) as i:
                    for b in range(2):
                        chunk(p, p * TILES + i * (2 * CT) + (b + 1) * CT, kv_round(p, i * 2 + b + 2), buf=b)
                chunk(p, p * TILES + (WHOLE - 1) * CT, kv_round(p, WHOLE), TAIL_K, 2)
                T = p * TILES + WHOLE * CT
                exps(T, 0)
                exps(T + 1, 1)
                kv_copies(p * ROUNDS + ROUNDS + 1, 0, CK, 0)
                exps(T + 2, 2, SR)
                q_copy(p * ROUNDS + ROUNDS + 2, 0)
                q_copy(p * ROUNDS + ROUNDS + 3, 1)

            act.wait_ge(tail_pe, 2)
            nc.scalar.activation(x2_t, sc1, ACT.Copy).then_inc(tail_act, 1)
            act.wait_ge(tail_pe, 3)
            nc.scalar.activation(logits[:, :, :], proj[:, 0, 0:LT * E].rearrange("p (j e) -> p j e", e=E),
                                 ACT.Copy).then_inc(tail_act, 1)
            act.wait_ge(tail_dve, 2)
            nc.scalar.activation(weight[:, 1, :], weight[:, 0, :], ACT.Exp).then_inc(tail_act, 1)

        @block.tensor
        def _(pe):
            mm, turn = nc.tensor.matmul, nc.tensor.transpose

            def turn_keys(k):
                pe.wait_ge(keys_normed, min((k * CT + CT - 1) // GC, ST // GC) + 1)
                if k >= 2:
                    pe.wait_ge(keys_copied, k - 1)
                for t in range(CT if k < WHOLE else TAIL_TILES):
                    j = k * CT + t
                    if j < ST:
                        last = turn(acc[:, k % 2, t * P:(t + 1) * P], keys_raw[:, j, :], ident)
                    else:
                        last = turn(acc[:, k % 2, t * P:t * P + SR], keys_last[:, :], ident[0:SR, 0:SR])
                last.then_inc(keys_turned, 1)

            def bias_row(view, row, j):
                mm(view, ones[0:1, :], row, start=True, stop=False)

            pe.wait_ge(x_in, 16)
            pe.wait_ge(pack_in, 16)
            for j in range(LT):
                last = turn(sc0[:, j * P:(j + 1) * P], x_sb[:, j, :], ident)
            last.then_inc(pe_step, 1)
            pe.wait_ge(conv_w_in, 18 * 16)
            for n in range(NH):
                last = mm(sc1[0:FO, n * HALF:(n + 1) * HALF], w_12[:, 0, :], pe_t[:, n * HALF:(n + 1) * HALF],
                          start=True, stop=True)
            last.then_inc(pe_step, 1)
            pe.wait_ge(act_step, act_did("x_t"))
            pe.wait_ge(ones_set, 1)
            for j in range(LT):
                bias_row(tiles(sc0)[:, j, :], b_v, j)
                last = mm(tiles(sc0)[:, j, :], x_t[:, j * P:(j + 1) * P], w_uv[:, 1, :], start=False, stop=True)
            last.then_inc(pe_step, 1)
            pe.wait_ge(act_step, act_did("h1"))
            for n in range(NH):
                last = mm(pj[0:FO, n * HALF:(n + 1) * HALF], w_12[:, 1, :], h1_t[:, n * HALF:(n + 1) * HALF],
                          start=True, stop=True)
            last.then_inc(pe_step, 1)
            pe.wait_ge(act_step, act_did("h2"))
            for n in range(NH):
                last = mm(pj[:, n * HALF:(n + 1) * HALF], w_uv[:, 0, :], x_t[:, n * HALF:(n + 1) * HALF],
                          start=True, stop=True)
            last.then_inc(pe_step, 1)
            for j in range(LT):
                bias_row(tiles(sc1)[:, j, :], b_h, j)
                last = mm(tiles(sc1)[:, j, :], h2_t[:, j * P:(j + 1) * P], w_3[:, :], start=False, stop=True)
            last.then_inc(pe_step, 1)
            for k in range(4):
                turn_keys(k)
            pe.wait_ge(dft_in, 32)
            pe.wait_ge(act_step, act_did("v"))
            COS0, COS1, SIN0, SIN1, COS_N, SIN_N = (slice(i * P, (i + 1) * P) for i in range(6))
            v_blocks = v_time.rearrange("p (b w) d -> p w b d", w=2)
            h_blocks = h_sb.rearrange("p (b w) d -> p w b d", w=2)
            for i, f in enumerate((COS0, COS1, SIN_N, SIN1)):
                if i == 2:
                    pe.wait_ge(dve_step, dve_did("h"))
                bank = scores[:, i // 2, i % 2, :].rearrange("p (b d) -> p b d", d=D)
                mm(bank, fwd[:, 0, f], v_blocks[:, 0, :, :], start=True, stop=False)
                mm(bank, fwd[:, 1, f], v_blocks[:, 1, :, :], start=False, stop=True).then_inc(pe_step, 1)
            pe.wait_ge(act_step, act_did("u"))
            for i, f in enumerate((COS0, COS1, SIN0, SIN1, COS_N)):
                if i >= 2:
                    pe.wait_ge(act_step, act_did(f"v_dft{i - 2}"))
                bank = (proj[:, i, :] if i < 2 else scores[:, (i - 2) // 2, (i - 2) % 2, :])
                bank = bank.rearrange("p (b d) -> p b d", d=D)
                mm(bank, fwd[:, 2, f], h_blocks[:, 0, :, :], start=True, stop=False)
                mm(bank[:, 1:NB, :], fwd[:, 0, f], h_blocks[:, 0, 0:NB - 1, :], start=False, stop=False)
                mm(bank[:, 1:NB, :], fwd[:, 1, f], h_blocks[:, 1, 0:NB - 1, :], start=False, stop=False)
                mm(bank, fwd[:, 3, f], h_blocks[:, 1, :, :], start=False, stop=True).then_inc(pe_step, 1)
            for k in range(4, WHOLE + 1):
                turn_keys(k)
            pe.wait_ge(act_step, act_did("h_dft4"))
            pe.wait_ge(dve_step, dve_did("spectrum"))
            for b in range(NB):
                for f in range(2 * 2):
                    y = (y_cos if f < 2 else y_sin)[:, f % 2, b, :]
                    last = mm(pj[:, b * BLK:(b + 1) * BLK], y, inv[:, f, :], start=(f == 0), stop=(f == 3))
            last.then_inc(pe_step, 1)
            pe.wait_ge(dve_step, dve_did("y"))
            for j in range(LT):
                bias_row(tiles(sc0)[:, j, :], b_o, j)
                last = mm(tiles(sc0)[:, j, :], y_t[:, j * P:(j + 1) * P], w_o[:, :], start=False, stop=True)
            last.then_inc(pe_step, 1)
            pe.wait_ge(dve_step, dve_did("lat"))
            for j in range(LT):
                last = turn(sc1[:, j * P:(j + 1) * P], lat[:, j, :], ident)
            last.then_inc(pe_step, 1)

            def project_kv(n, src, vt=CT):
                pe.wait_ge(act_round, n - 1)
                pe.wait_ge(dve_round, n - 1)
                whole = vt if vt == CT else vt - 1
                width = src.shape[1]
                mm(proj[:, 0, 0:width], w_kv[:, 0, :], src, start=True, stop=True)
                for t in range(whole):
                    last = mm(proj[:, 1, t * P:(t + 1) * P], src[:, t * P:(t + 1) * P], w_kv[:, 1, :],
                              start=True, stop=True)
                if whole < vt:
                    last = mm(proj[0:SR, 1, whole * P:vt * P], src[:, whole * P:whole * P + SR], w_kv[:, 1, :],
                              start=True, stop=True)
                last.then_inc(proj_ready, 1)

            def project_q(n, h):
                pe.wait_ge(act_round, n - 1)
                pe.wait_ge(dve_round, n - 1)
                for m in range(NH):
                    last = mm(proj[:, m, :], w_q[:, h, :, :].rearrange("d c n -> d (c n)"),
                              lat_t[:, m * HALF:(m + 1) * HALF], start=True, stop=True)
                last.then_inc(proj_ready, 1)

            def qk(T, k):
                for n in range(NH):
                    pe.wait_ge(exp_done, T * 2 + n + 1)
                    for h in range(2):
                        for part in range(2):
                            last = mm(scores[:, n, h, :], k[:, h, :], q_parts[:, h, part, n * HALF:(n + 1) * HALF],
                                      start=(part == 0), stop=(part == 1))
                    last.then_inc(scores_ready, 1)

            def pv(T, slot, v, first=False, final=False, rows=P):
                pe.wait_ge(clip_done, T + 1)
                for n in range(NH):
                    for h in range(2):
                        r = slice(h * DH, (h + 1) * DH)
                        last = mm(acc[r, n, :], v[0:rows, r], probs[0:rows, slot, n, h, :],
                                  start=first, stop=final)
                last.then_inc(pv_done, 1)

            def k_of(buf, t):
                return k_parts[:, buf, :, t * P:(t + 1) * P] if buf < 2 else k_tail[:, :, t * P:(t + 1) * P]

            def chunk(p, T, buf, n, src, vt=CT, stage_wait=None, opening=False):
                pe.wait_ge(act_round, n - 1)
                pe.wait_ge(dve_round, n - 1)
                for t in range(CT):
                    qk(T + t, k_of(buf, t))
                    if t >= LAG:
                        if opening and t == LAG:
                            pe.wait_ge(heads_done, p + 1)
                        pv(T + (t - LAG), t - LAG, v_sb[:, buf, t - LAG, :], first=(opening and t == LAG))
                    elif not opening:
                        pv(T + t - LAG, CT - LAG + t, v_sb[:, 1 - buf, CT - LAG + t, :])
                    if t == 1:
                        if opening:
                            pe.wait_ge(den_read, p + 1)
                        if stage_wait is not None:
                            pe.wait_ge(*stage_wait)
                        project_kv(n, src, vt)

            pe.wait_ge(keys_copied, WHOLE + 1)
            pe.wait_ge(weights_in, 48)
            mm(proj[:, 0, :], w_kv[:, 0, :], keys_t[:, 0:CK], start=True, stop=True).then_inc(pv_done, PREV_SLOTS)
            mm(proj[:, 1, 0:P], keys_t[:, 0:P], w_kv[:, 1, :], start=True, stop=True).then_inc(den_ready, 1)
            for t in range(1, CT):
                last = mm(proj[:, 1, t * P:(t + 1) * P], keys_t[:, t * P:(t + 1) * P], w_kv[:, 1, :],
                          start=True, stop=True)
            last.then_inc(proj_ready, 1)
            pe.wait_ge(act_step, act_did("lat_t"))
            project_q(2, 0)
            project_q(3, 1)
            with pe.Fori(0, pairs) as p:
                chunk(p, p * TILES, 0, kv_round(p, 1), keys_t[:, CK:2 * CK], opening=True)
                pairs_done = p * ((WHOLE - 2) // 2)
                with pe.Fori(0, (WHOLE - 2) // 2) as i:
                    for b in range(2):
                        chunk(p, p * TILES + i * (2 * CT) + (b + 1) * CT, 1 - b, kv_round(p, i * 2 + b + 2),
                              stage[:, b, :], stage_wait=(stage_in[b], (pairs_done + i) * 16 + 16))
                chunk(p, p * TILES + (WHOLE - 1) * CT, 1, kv_round(p, WHOLE), keys_t[:, WHOLE * CK:S], vt=TAIL_TILES)
                T = p * TILES + WHOLE * CT
                pe.wait_ge(act_round, kv_round(p, WHOLE))
                pe.wait_ge(dve_round, kv_round(p, WHOLE))
                qk(T, k_of(2, 0))
                pv(T - 2, 2, v_sb[:, 1, 2, :])
                qk(T + 1, k_of(2, 1))
                pv(T - 1, 3, v_sb[:, 1, 3, :])
                pe.wait_ge(weights_in, p * 48 + 96)
                project_kv(p * ROUNDS + ROUNDS + 1, keys_t[:, 0:CK])
                qk(T + 2, k_of(2, 2))
                pv(T, 0, v_tail[:, 0, :])
                project_q(p * ROUNDS + ROUNDS + 2, 0)
                pv(T + 1, 1, v_tail[:, 1, :])
                project_q(p * ROUNDS + ROUNDS + 3, 1)
                pv(T + 2, 2, v_tail[:, 2, :], final=True, rows=SR)
                pe.wait_ge(act_round, p * ROUNDS + ROUNDS + 3)
                pe.wait_ge(dve_round, p * ROUNDS + ROUNDS + 3)
                pe.wait_ge(sum_done, p * TILES + TILES + PREV_SLOTS)
                for n in range(NH):
                    for h in range(2):
                        last = mm(proj[h * DH:(h + 1) * DH, n, :], ones[:, 0:DH], sums[:, n, h, :],
                                  start=True, stop=True)
                last.then_inc(den_ready, 1)

            pe.wait_ge(heads_done, pairs + 1)
            pe.wait_ge(late_in, 48)
            for j in range(LT):
                bias_row(tiles(sc0)[:, j, :], b_x, j)
                for g in range(pairs):
                    last = mm(tiles(sc0)[:, j, :], heads_t[:, g, j * P:(j + 1) * P], w_xo[:, g, :],
                              start=False, stop=(g == pairs - 1))
            last.then_inc(tail_pe, 1)
            pe.wait_ge(tail_dve, 1)
            for j in range(LT):
                last = turn(sc1[:, j * P:(j + 1) * P], x2[:, j, :], ident)
            last.then_inc(tail_pe, 1)
            pe.wait_ge(tail_act, 1)
            for j in range(LT):
                last = mm(proj[:, 0, j * E:(j + 1) * E], x2_t[:, j * P:(j + 1) * P], w_router[:, :],
                          start=True, stop=True)
            last.then_inc(tail_pe, 1)
            pe.wait_ge(tail_dve, 3)
            mm(proj[:, 1, 0:LT * E], earlier, chosen_pad[:, LT * E:], start=True, stop=False)
            for i in range(1, LT):
                last = mm(proj[:, 1, 0:LT * E], ones[:, :], chosen_pad[:, (LT - i) * E:(2 * LT - i) * E],
                          start=False, stop=(i == LT - 1))
            last.then_inc(tail_pe, 1)
            banks = [scores[:, 0, :, :], scores[:, 1, :, :]]
            experts = w_experts[:, :, :].rearrange("d e f -> d (e f)")
            for j in range(LT):
                if j >= 2:
                    pe.wait_ge(moe_added, j - 1)
                for n in range(2):
                    last = mm(banks[j % 2][:, n, :], x2_t[:, j * P:(j + 1) * P],
                              experts[:, n * HALF:(n + 1) * HALF], start=True, stop=True)
                last.then_inc(moe_ready, 1)

        @block.vector
        def _(dve):
            v = nc.vector
            links = 0

            def link(ins):
                nonlocal links
                links += 1
                ins.then_inc(dve_link, 1)
                dve.wait_ge(dve_link, links)

            v.memset(ones[:, :], 1.0).then_inc(ones_set, 1)

            def key_statistics(g):
                dve.wait_ge(key_in[g], 16)
                for j in range(g * GC, (g + 1) * GC):
                    last = v.bn_stats(key_stat[:, j, :], keys_raw[:, j, :])
                link(last)
                for j in range(g * GC, (g + 1) * GC):
                    last = v.bn_aggr(key_mv[:, j, :], key_stat[:, j, :])
                last.then_inc(key_stats, 1)

            def key_norm(g):
                dve.wait_ge(key_stats, g + 1)
                dve.wait_ge(key_rstds, g + 1)
                for j in range(g * GC, (g + 1) * GC):
                    last = v.tensor_scalar(keys_raw[:, j, :], keys_raw[:, j, :], key_mv[:, j, 0:1],
                                           key_rstd[:, j:j + 1], ALU.subtract, ALU.mult)
                last.then_inc(keys_normed, 1)

            key_statistics(0)
            key_statistics(1)
            key_norm(0)
            dve.wait_ge(pe_step, pe_did("h3"))
            for j in range(LT):
                last = v.tensor_scalar(h_sb[:, j, :], tiles(sc1)[:, j, :], decay[:, j:j + 1], None, ALU.mult)
            last.then_inc(dve_step, 1)
            key_norm(1)
            for g in range(2, ST // GC):
                key_statistics(g)
                key_norm(g)
            dve.wait_ge(last_key_in, 16)
            link(v.bn_stats(key_stat[0:SR, ST, :], keys_last[:, :]))
            v.bn_aggr(key_mv[0:SR, ST, :], key_stat[0:SR, ST, :]).then_inc(key_stats, 1)
            dve.wait_ge(key_stats, ST // GC + 1)
            dve.wait_ge(key_rstds, ST // GC + 1)
            v.tensor_scalar(keys_last[:, :], keys_last[:, :], key_mv[0:SR, ST, 0:1], key_rstd[0:SR, ST:TILES],
                            ALU.subtract, ALU.mult).then_inc(keys_normed, 1)

            dve.wait_ge(act_step, act_did("h_dft4"))
            link(v.tensor_copy(h_cos_n[:, 1, :, :], h_cos[:, 1, :, :]))
            dve.wait_ge(keys_turned, 4)
            for d in range(NB):
                n = NB - d

                def window(t):
                    return t[:, :, d:d + 1, :].broadcast_to([P, 2, n, D])

                for to, first, second, op in ((y_cos, (v_cos, h_cos), (v_sin, h_sin), ALU.subtract),
                                              (y_sin, (v_cos, h_sin), (v_sin, h_cos_n), ALU.add)):
                    to = to[:, :, d:NB, :]
                    pa, pb = product_a[:, :, 0:n, :], product_b[:, :, 0:n, :]
                    v.tensor_tensor(pa if d else to, first[0][:, :, 0:n, :], window(first[1]), ALU.mult)
                    link(v.tensor_tensor(pb, second[0][:, :, 0:n, :], window(second[1]), ALU.mult))
                    if d:
                        link(v.tensor_tensor(to, to, pa, ALU.add))
                    last = v.tensor_tensor(to, to, pb, op)
                    if d < NB - 1 or op == ALU.subtract:
                        link(last)
            last.then_inc(dve_step, 1)
            dve.wait_ge(pe_step, pe_did("conv"))
            v.tensor_tensor(y_t, u_t, pj, ALU.mult).then_inc(dve_step, 1)

            norms = 0

            def layernorm(to, frm):
                nonlocal norms
                norms += 1
                for j in range(LT):
                    last = v.bn_stats(row_stat[:, j, :], frm[:, j, :])
                link(last)
                for j in range(LT):
                    last = v.bn_aggr(row_mv[:, j, :], row_stat[:, j, :])
                last.then_inc(row_stats, 1)
                dve.wait_ge(row_stats, norms)
                dve.wait_ge(row_rstds, norms)
                for j in range(LT):
                    last = v.tensor_scalar(to[:, j, :], frm[:, j, :], row_mv[:, j, 0:1], row_rstd[:, j:j + 1],
                                           ALU.subtract, ALU.mult)
                return last

            dve.wait_ge(pe_step, pe_did("attn"))
            v.tensor_tensor(resid, x_sb[:, :, :], tiles(sc0), ALU.add).then_inc(dve_step, 1)
            dve.wait_ge(dve_step, dve_did("resid"))
            link(layernorm(x1, resid))
            layernorm(lat, x1).then_inc(dve_step, 1)
            v.memset(scratch[:, 4:5], 0.0).then_inc(sum_done, PREV_SLOTS)
            v.memset(scratch[:, 5:6], 0.0).then_inc(heads_done, 1)
            v.memset(scratch[:, 6:7], 0.0).then_inc(den_read, 1)

            def k_low(n, buf, width):
                dve.wait_ge(act_round, n)
                dst = k_parts[:, buf, :, :] if buf < 2 else k_tail[:, :, :]
                for h in range(2):
                    r, other = slice(h * DH, (h + 1) * DH), slice((1 - h) * DH, (2 - h) * DH)
                    last = v.tensor_tensor(dst[other, h, 0:width], proj[r, 0, 0:width],
                                           dst[r, h, 0:width].bitcast(F32), ALU.subtract)
                last.then_inc(dve_round, 1)

            def q_low(n, h):
                dve.wait_ge(act_round, n)
                v.tensor_tensor(q_parts[:, h, 1, :], pj, q_parts[:, h, 0, :].bitcast(F32), ALU.subtract)\
                    .then_inc(dve_round, 1)

            def clip_and_sum(T, slot, rows=P, first=None):
                tile = probs[0:rows, slot, :, :, :]
                dve.wait_ge(exp_done, T * 2 + NH + 2)
                v.tensor_scalar(tile, tile, float(np.exp(CLIP)), float(np.exp(-CLIP)), ALU.min, ALU.max)\
                    .then_inc(clip_done, 1)
                dve.wait_ge(clip_done, T + 1)
                dve.wait_ge(sum_done, T + PREV_SLOTS)
                if first is not None:
                    dve.wait_ge(den_ready, first + 1)
                    v.tensor_copy(sums[:, :, :, :], tile).then_inc(sum_done, 1)
                else:
                    v.tensor_tensor(sums[0:rows, :, :, :], sums[0:rows, :, :, :], tile, ALU.add)\
                        .then_inc(sum_done, 1)

            def chunk(p, T, n, width=CK, buf=0, opening=False):
                clip_and_sum(T, 0, first=p if opening else None)
                clip_and_sum(T + 1, 1)
                k_low(n, buf, width)
                clip_and_sum(T + 2, 2)
                clip_and_sum(T + 3, 3)

            k_low(1, 0, CK)
            q_low(2, 0)
            q_low(3, 1)
            with dve.Fori(0, pairs) as p:
                chunk(p, p * TILES, kv_round(p, 1), buf=1, opening=True)
                with dve.Fori(0, (WHOLE - 2) // 2) as i:
                    for b in range(2):
                        chunk(p, p * TILES + i * (2 * CT) + (b + 1) * CT, kv_round(p, i * 2 + b + 2), buf=b)
                chunk(p, p * TILES + (WHOLE - 1) * CT, kv_round(p, WHOLE), TAIL_K, 2)
                T = p * TILES + WHOLE * CT
                clip_and_sum(T, 0)
                clip_and_sum(T + 1, 1)
                k_low(p * ROUNDS + ROUNDS + 1, 0, CK)
                clip_and_sum(T + 2, 2, SR)
                q_low(p * ROUNDS + ROUNDS + 2, 0)
                q_low(p * ROUNDS + ROUNDS + 3, 1)
                dve.wait_ge(den_ready, p + 2)
                v.reciprocal(recip[:, :, :], proj[:, :, :]).then_inc(den_read, 1)
                dve.wait_ge(den_read, p + 2)
                dve.wait_ge(pv_done, p * TILES + TILES + PREV_SLOTS)
                v.tensor_tensor(heads_flat[:, bass.ds(p * L, L)], ac, recip[:, :, :].rearrange("p n q -> p (n q)"),
                                ALU.mult).then_inc(heads_done, 1)

            dve.wait_ge(tail_pe, 1)
            link(v.tensor_tensor(moe, x1[:, :, :], tiles(sc0), ALU.add))
            layernorm(x2, moe).then_inc(tail_dve, 1)
            dve.wait_ge(tail_act, 2)
            for j in range(LT):
                last = v.max(top[:, j, :], logits[:, j, :])
            link(last)
            for j in range(LT):
                last = v.max_index(top_at[:, j, :], top[:, j, :], logits[:, j, :])
            link(last)
            v.tensor_tensor(weight[:, 0, :], top[:, :, 1], top[:, :, 0], ALU.subtract).then_inc(tail_dve, 1)
            link(v.tensor_copy(top_no[:, :, :], top_at[:, :, :]))
            one, two = gate_one, gate_two
            v.memset(chosen_pad[:, 0:LT * E], 0.0)
            v.tensor_tensor(one, expert_no, top_no[:, :, 0:1].broadcast_to([P, LT, E]), ALU.is_equal)
            link(v.tensor_tensor(two, expert_no, top_no[:, :, 1:2].broadcast_to([P, LT, E]), ALU.is_equal))
            v.tensor_tensor(chosen, one, two, ALU.add).then_inc(tail_dve, 1)
            dve.wait_ge(tail_act, 3)
            link(v.tensor_scalar(weight[:, 2, :], weight[:, 1, :], 1.0, None, ALU.add))
            link(v.reciprocal(weight[:, 2, :], weight[:, 2, :]))
            link(v.tensor_tensor(weight[:, 3, :], weight[:, 1, :], weight[:, 2, :], ALU.mult))

            def per_tile(i):
                return weight[:, i, :].rearrange("p (j o) -> p j o", o=1).broadcast_to([P, LT, E])

            v.tensor_tensor(one, one, per_tile(2), ALU.mult)
            link(v.tensor_tensor(two, two, per_tile(3), ALU.mult))
            v.tensor_tensor(one, one, two, ALU.add)
            dve.wait_ge(tail_pe, 4)
            link(v.tensor_scalar(kept, proj[:, 1, 0:LT * E].rearrange("p (j e) -> p j e", e=E), float(CAP), None,
                                 ALU.is_lt))
            link(v.tensor_tensor(one, one, kept, ALU.mult))
            for j in range(LT):
                dve.wait_ge(moe_ready, j + 1)
                for e in range(E):
                    view = scores[:, j % 2, e // 4, (e % 4) * D:(e % 4 + 1) * D]
                    last = v.scalar_tensor_tensor(out=x3[:, j, :], in0=view, scalar=one[:, j, e:e + 1],
                                                  in1=(x3 if e else x2)[:, j, :], op0=ALU.mult, op1=ALU.add)
                    if e < E - 1:
                        link(last)
                last.then_inc(moe_added, 1)
            dve.wait_ge(moe_added, LT)
            layernorm(moe, x3).then_inc(tail_dve, 2)


_INS = ["x", "ctx_1024", "L0_attn_Wu", "L0_attn_bu", "L0_attn_Wv", "L0_attn_bv", "L0_attn_W1", "L0_attn_b1",
        "L0_attn_W2", "L0_attn_b2", "L0_attn_W3", "L0_attn_b3", "L0_attn_Wo", "L0_attn_bo", "L0_xattn_ln_l_w",
        "L0_xattn_ln_l_b", "L0_xattn_ln_c_w", "L0_xattn_ln_c_b", "L0_xattn_Wq", "L0_xattn_Wkv", "L0_xattn_Wo",
        "L0_xattn_bo", "L0_ffn_We"]


def kernel(**inputs):
    from concourse import bacc
    from concourse.bass_utils import run_bass_kernel_spmd

    arrays = {n: np.ascontiguousarray(inputs[n]) for n in _INS}
    arrays["router_t"] = np.ascontiguousarray(np.asarray(inputs["L0_ffn_Wr"]).T)
    arrays.update(constants())
    nc = bacc.Bacc("TRN2", target_bir_lowering=False, num_devices=1)
    aps = {n: nc.dram_tensor(f"in_{n}", v.shape, mybir.dt.from_np(v.dtype), kind="ExternalInput").ap()
           for n, v in arrays.items()}
    out = nc.dram_tensor("out", (1, L, D), F32, kind="ExternalOutput").ap()
    build(nc, aps, out)
    r = run_bass_kernel_spmd(nc, [{f"in_{n}": v for n, v in arrays.items()}], core_ids=[0])
    return r.results[0]["out"]
```

```python
from contextlib import ExitStack

import numpy as np

import concourse.bass as bass
from concourse import mybir

F32 = mybir.dt.float32
F32R = mybir.dt.float32r
U32 = mybir.dt.uint32
ALU = mybir.AluOpType
ACT = mybir.ActivationFunctionType

P = 128
D = 128
L = 1024
LT = L // P
NH = 2
HT = LT // NH
HALF = L // NH
S = 6404
ST = S // P
SR = S - ST * P
TILES = ST + 1
H = 16
DH = 64
PAIRS = H // 2
CT = 4
CK = CT * P
WHOLE = ST // CT
TAIL_TILES = TILES - WHOLE * CT
TAIL_K = TAIL_TILES * P
PADDED = WHOLE * CK + TAIL_K
GC = 10
E = 8
CAP = int(L * 2 / E * 1.5) + 1
FO = 64
BLK = 256
NB = L // BLK
W = 2 * BLK
CLIP = 11.0
EPS = 1e-5
SCALE = DH ** -0.5
ROUNDS = WHOLE + 1 + 2
PIECES = (WHOLE - 2) // 2 + 3
LAG = 2
PREV_SLOTS = 3


def constants():
    ident = np.eye(P)
    earlier = np.triu(np.ones((P, P)), 1)
    expert = np.tile(np.arange(E), (P, LT))
    t = np.arange(L)
    decay = np.exp(np.float32(-0.01) * t.astype(np.float32)).reshape(LT, P).T
    pack = np.concatenate([ident, earlier, expert, decay], 1).astype(np.float32)

    div = np.exp(np.arange(0, FO, 2, dtype=np.float32) * np.float32(-(np.log(10000.0) / FO)))
    ang = t.astype(np.float32)[:, None] * div.astype(np.float32)
    pe = np.zeros((L, FO), np.float32)
    pe[:, 0::2], pe[:, 1::2] = np.sin(ang), np.cos(ang)

    n, k = np.arange(W)[:, None], np.arange(BLK)[None, :]
    cos, sin = np.cos(2 * np.pi * n * k / W), np.sin(2 * np.pi * n * k / W)
    nyquist = np.cos(np.pi * n)
    sin_n = sin.copy()
    sin_n[:, :1] = nyquist
    forward = np.concatenate([cos, sin_n], 1)
    inv_cos = 2 * cos[BLK:].T / W
    inv_cos[0] /= 2
    inv_sin = 2 * sin[BLK:].T / W
    inv_sin[0] = nyquist[BLK:, 0] / W
    inverse = np.concatenate([inv_cos, inv_sin], 0)
    return {"c_pack": pack, "c_pe": np.ascontiguousarray(pe.T),
            "c_fwd": forward.astype(np.float32), "c_inv": inverse.astype(np.float32)}


def build(nc, a, out, pairs=PAIRS, probe=None):
    ctx = ExitStack()
    with ctx:
        def sb(name, shape, dt=F32):
            return ctx.enter_context(nc.sbuf_tensor(name, shape, dt))

        def sem(name):
            return ctx.enter_context(nc.semaphore(name))

        pack = sb("pack", [P, 2 * P + LT * E + LT + 7])
        ident, earlier = pack[:, 0:P], pack[:, P:2 * P]
        expert_no = pack[:, 2 * P:2 * P + LT * E].rearrange("p (j e) -> p j e", e=E)
        decay = pack[:, 2 * P + LT * E:2 * P + LT * E + LT]
        bu_col, b1_col, b2_col, lw_col, lb_col, cw_col, cb_col = (
            pack[:, 2 * P + LT * E + LT + i:2 * P + LT * E + LT + i + 1] for i in range(7))
        ones = sb("ones", [P, P])
        bias_rows = sb("bias_rows", [1, 4, D])
        b_v, b_h, b_o, b_x = (bias_rows[0:1, i, :] for i in range(4))
        w_filter = sb("w_filter", [FO, 2 * FO + D])
        w_1, w_2, w_3 = (w_filter[:, i:j] for i, j in ((0, FO), (FO, 2 * FO), (2 * FO, 2 * FO + D)))
        w_router = sb("w_router", [P, E])
        w_experts = sb("w_experts", [P, E, D])
        w_xo = sb("w_xo", [P, PAIRS, D])
        w_next = sb("w_next", [P, 4, P])
        w_pair = sb("w_pair", [P, 4, P])
        keys_t = sb("keys_t", [P, PADDED])
        stage = sb("stage", [P, 2, CK])
        k_parts = sb("k_parts", [P, 2, 2, CK], F32R)
        k_tail = sb("k_tail", [P, 2, TAIL_TILES * P], F32R)
        v_tail = sb("v_tail", [P, TAIL_TILES, P])
        q_parts = sb("q_parts", [P, 2, 2, L], F32R)
        lat_t = sb("lat_t", [P, L])
        probs = sb("probs", [P, CT, NH, 2, HALF])
        heads_t = sb("heads_t", [P, PAIRS, L])
        x1 = sb("x1", [P, LT, D])
        scratch = sb("scratch", [P, 8])

        keys_raw = sb("keys_raw", [P, ST, D])
        keys_last = sb("keys_last", [SR, D])

        def carve(t, at, shape):
            n = int(np.prod(shape[1:]))
            view = t[0:shape[0], at:at + n]
            if len(shape) == 3:
                view = view.rearrange("p (a b) -> p a b", b=shape[2])
            if len(shape) == 4:
                view = view.rearrange("p (a b c) -> p a b c", b=shape[2], c=shape[3])
            return view

        flat = probs[:, :, :, :, :].rearrange("p a b c d -> p (a b c d)")
        raw_flat = keys_raw[:, :, :].rearrange("p a b -> p (a b)")
        sums = carve(raw_flat, 2 * L, [P, NH, 2, HALF])
        unscaled = carve(raw_flat, 4 * L, [P, NH, HALF])
        den = carve(raw_flat, 0, [P, L])
        v_sb = carve(raw_flat, 5 * L, [P, 2, CT, P])
        heads_flat = heads_t[:, :, :].rearrange("p a b -> p (a b)")
        x_t = carve(heads_flat, 0, [P, L])
        h1_t = carve(heads_flat, L, [FO, L])
        h2_t = carve(heads_flat, 2 * L, [FO, L])
        h_sb = carve(heads_flat, 3 * L, [P, LT, D])
        v_time = carve(heads_flat, 4 * L, [P, LT, D])
        u_t = carve(heads_flat, 5 * L, [P, L])
        inv = carve(heads_flat, 7 * L, [P, W // P, BLK])
        y_cos = carve(heads_flat, 0, [P, 2, NB, D])
        y_sin = carve(heads_flat, L, [P, 2, NB, D])
        product_a = carve(heads_flat, 2 * L, [P, 2, NB, D])
        y_t = carve(heads_flat, 3 * L, [P, L])
        product_b = carve(heads_flat, 4 * L, [P, 2, NB, D])
        v_cos = carve(flat, 0, [P, 2, NB, D])
        v_sin = carve(flat, L, [P, 2, NB, D])
        h_cos = carve(flat, 2 * L, [P, 2, NB, D])
        h_sin = carve(flat, 3 * L, [P, 2, NB, D])
        h_cos_n = carve(flat, 4 * L, [P, 2, NB, D])
        fwd = carve(flat, 5 * L, [P, W // P, 2 * BLK])
        x_sb = carve(flat, 7 * L, [P, LT, D])
        w_uvo = v_tail
        pe_t = x1[0:FO, :, :].rearrange("p a b -> p (a b)")
        resid = carve(flat, 0, [P, LT, D])

        key_stat = sb("key_stat", [P, TILES, 6])
        key_mv = sb("key_mv", [P, TILES, 2])
        key_rstd = sb("key_rstd", [P, TILES])
        half_neg = sb("half_neg", [P, TILES])
        row_stat = sb("row_stat", [P, 4, LT, 6])
        row_mv = sb("row_mv", [P, 4, LT, 2])
        row_rstd = sb("row_rstd", [P, 4, LT])

        lat = keys_raw[:, 8:16, :]
        x2 = carve(flat, 0, [P, LT, D])
        x2_t = carve(flat, L, [P, L])
        x3 = carve(flat, 2 * L, [P, LT, D])
        moe = carve(flat, 3 * L, [P, LT, D])
        small = carve(flat, 4 * L, [P, 5 * LT * E])
        gate_one, gate_two, kept, chosen = (small[:, i * LT * E:(i + 1) * LT * E].rearrange("p (j e) -> p j e", e=E)
                                            for i in (0, 1, 2, 4))
        chosen_pad = small[:, 3 * LT * E:5 * LT * E]
        logits, top, top_no = (carve(flat, 5 * L + i * LT * E, [P, LT, E]) for i in range(3))
        top_at = sb("top_at", [P, LT, E], U32)
        weight = carve(flat, 5 * L + 3 * LT * E, [P, 4, LT])

        scores = ctx.enter_context(nc.psum_tensor("scores", [P, NH, 2, HALF], F32))
        acc = ctx.enter_context(nc.psum_tensor("acc", [P, NH, HALF], F32))
        proj = ctx.enter_context(nc.psum_tensor("proj", [P, 2, HALF], F32))
        sc0 = scores[:, 0, :, :].rearrange("p b n -> p (b n)")
        sc1 = scores[:, 1, :, :].rearrange("p b n -> p (b n)")
        pj = proj[:, :, :].rearrange("p b n -> p (b n)")
        q_bank = [pj, sc0]
        ac = acc[:, :, :].rearrange("p b n -> p (b n)")

        conv_bank = [bank[:, 0:BLK] for bank in (proj[:, 0, :], proj[:, 1, :], scores[:, 1, 0, :], scores[:, 1, 1, :])]

        def tiles(view):
            return view.rearrange("p (j d) -> p j d", d=D)

        x_in, pack_in, filter_in, conv_w_in, dft_in, late_in = (
            sem(n) for n in ("x_in", "pack_in", "filter_in", "conv_w_in", "dft_in", "late_in"))
        key_in = [sem(f"key_in{g}") for g in range(ST // GC)]
        last_key_in = sem("last_key_in")
        ones_set = sem("ones_set")
        key_stats, key_rstds, keys_normed = sem("key_stats"), sem("key_rstds"), sem("keys_normed")
        keys_turned, keys_copied = sem("keys_turned"), sem("keys_copied")
        pad_set = sem("pad_set")
        pe_step, act_step = sem("pe_step"), sem("act_step")
        dve_link, pool_link = sem("dve_link"), sem("pool_link")
        row_stats, row_rstds = sem("row_stats"), sem("row_rstds")
        weights_in, weights_copied = sem("weights_in"), sem("weights_copied")
        stage_in = [sem("stage_in0"), sem("stage_in1")]
        proj_ready, act_round, dve_round = sem("proj_ready"), sem("act_round"), sem("dve_round")
        den_ready, pair_copied, inverted, heads_done = (
            sem(n) for n in ("den_ready", "pair_copied", "inverted", "heads_done"))
        spectrum_done, conv_ready, y_done = sem("spectrum_done"), sem("conv_ready"), sem("y_done")
        attn_ready, lat_ready, lat_turned, lat_copied = (
            sem(n) for n in ("attn_ready", "lat_ready", "lat_turned", "lat_copied"))
        scores_ready, exp_done, clip_done = sem("scores_ready"), sem("exp_done"), sem("clip_done")
        sum_done, pv_done = sem("sum_done"), sem("pv_done")
        out_ready, x2_ready, x2_turned, x2_copied, logits_ready, logits_copied = (
            sem(n) for n in ("out_ready", "x2_ready", "x2_turned", "x2_copied", "logits_ready", "logits_copied"))
        out_read, gap_ready, gap_exp, chosen_ready, places_ready, final_ready = (
            sem(n) for n in ("out_read", "gap_ready", "gap_exp", "chosen_ready", "places_ready", "final_ready"))
        moe_ready, moe_added = sem("moe_ready"), sem("moe_added")
        stored = sem("stored")

        PE_STEPS = ["h1", "x_t", "h2", "v", "h3", "u", "v_dft0", "v_dft1", "v_dft2", "v_dft3",
                    "h_dft0", "h_dft1", "h_dft2", "h_dft3"]
        ACT_STEPS = ["h1", "x_t", "h2", "v", "h3", "u", "v_dft0", "v_dft1", "v_dft2", "v_dft3",
                     "h_dft0", "h_dft1", "h_dft2", "h_dft3"]

        def pe_did(name):
            return PE_STEPS.index(name) + 1

        def act_did(name):
            return ACT_STEPS.index(name) + 1

        def kv_round(p, c):
            return p * ROUNDS + c + 3

        block = ctx.enter_context(nc.Block())

        @block.sync
        def _(sp):
            sp.dma_start(x_sb[:, :, :], a["x"].rearrange("b (j p) d -> p (b j) d", p=P)).then_inc(x_in, 16)
            keys = a["ctx_1024"][0, 0:ST * P, :].rearrange("(p j) d -> p j d", j=ST)
            for g in range(ST // GC):
                sp.dma_start(keys_raw[:, g * GC:(g + 1) * GC, :], keys[:, g * GC:(g + 1) * GC, :])\
                    .then_inc(key_in[g], 16)
            sp.dma_start(keys_last[:, :], a["ctx_1024"][0, ST * P:S, :]).then_inc(last_key_in, 16)

            wkv = a["L0_xattn_Wkv"].rearrange("d (two n) -> d two n", two=2)

            def load_weights(p):
                sp.dma_start(w_next[:, 0:2, :], wkv[:, :, bass.ds(p * P, P)]).then_inc(weights_in, 16)
                for copy in range(2):
                    wq = a["L0_xattn_Wq"][:, bass.ds(p * P, P)].rearrange("d (h n) -> d h n", h=2)
                    sp.dma_start(w_next[:, 2:4, copy * DH:(copy + 1) * DH], wq).then_inc(weights_in, 16)

            load_weights(0)
            sp.dma_start(w_experts[:, :, :], a["L0_ffn_We"].rearrange("e d f -> d e f")).then_inc(late_in, 16)
            sp.dma_start(w_xo[:, :, :], a["L0_xattn_Wo"].rearrange("(g p) d -> p g d", p=P)).then_inc(late_in, 16)
            sp.dma_start(w_router[:, :], a["router_t"]).then_inc(late_in, 16)
            sp.wait_ge(keys_copied, WHOLE + 1)
            with sp.Fori(0, pairs) as p:
                sp.wait_ge(weights_copied, p + 1)
                load_weights((p + 1) % pairs)
                with sp.Fori(0, (WHOLE - 2) // 2) as i:
                    for b in range(2):
                        sp.wait_ge(proj_ready, kv_round(p, i * 2 + b))
                        sp.dma_start(stage[:, b, :], keys_t[:, bass.ds(i * (2 * CK) + (b + 2) * CK, CK)])\
                            .then_inc(stage_in[b], 16)
            for g in range(NH):
                sp.wait_ge(final_ready, g + 1)
                sp.dma_start(out[0, g * HALF:(g + 1) * HALF, :].rearrange("(j p) d -> p j d", p=P),
                             moe[:, g * HT:(g + 1) * HT, :]).then_inc(stored, 16)
            sp.wait_ge(stored, 32)

        @block.gpsimd
        def _(pool):
            pool.memset(half_neg[:, :], -0.5)
            pool.memset(keys_t[:, S:PADDED], 0.0).then_inc(pad_set, 1)
            links = 0

            def rstd(to, mv):
                nonlocal links
                pool.tensor_scalar(to, mv, EPS, None, ALU.add).then_inc(pool_link, 1)
                links += 1
                pool.wait_ge(pool_link, links)
                return pool.tensor_tensor(to, to, half_neg[0:to.shape[0], 0:to.shape[1]], ALU.pow)

            pool.wait_ge(pad_set, 1)
            for g in range(ST // GC):
                pool.wait_ge(key_stats, g + 1)
                span = slice(g * GC, (g + 1) * GC)
                rstd(key_rstd[:, span], key_mv[:, span, 1]).then_inc(key_rstds, 1)
            pool.wait_ge(key_stats, ST // GC + 1)
            rstd(key_rstd[0:SR, ST:TILES], key_mv[0:SR, ST:TILES, 1]).then_inc(key_rstds, 1)
            for n in range(4 * NH):
                norm, span = n // NH, slice(n % NH * HT, (n % NH + 1) * HT)
                pool.wait_ge(row_stats, n + 1)
                rstd(row_rstd[:, norm, span], row_mv[:, norm, span, 1]).then_inc(row_rstds, 1)

        @block.scalar
        def _(act):
            act.dma_start(pe_t, a["c_pe"]).then_inc(filter_in, 16)
            act.dma_start(w_filter[:, :], a["filter_pack"]).then_inc(filter_in, 16)
            act.dma_start(pack[:, :], a["const_pack"]).then_inc(pack_in, 16)
            act.dma_start(w_uvo[:, :, :], a["conv_pack"].rearrange("n d e -> d n e")).then_inc(conv_w_in, 16)
            act.dma_start(bias_rows[0:1, :, :], a["row_pack"].rearrange("(o n) d -> o n d", o=1)).then_inc(conv_w_in, 16)
            act.dma_start(fwd[:, :, :], a["c_fwd"].rearrange("(w p) k -> p w k", p=P)).then_inc(dft_in, 16)
            act.dma_start(inv[:, :, :], a["c_inv"].rearrange("(w p) k -> p w k", p=P)).then_inc(dft_in, 16)

            def copy(to, frm, step):
                act.wait_ge(pe_step, pe_did(step))
                nc.scalar.activation(to, frm, ACT.Copy).then_inc(act_step, 1)

            def turn_keys(k):
                n = CK if k < WHOLE else S - WHOLE * CK
                act.wait_ge(keys_turned, k + 1)
                nc.scalar.activation(keys_t[:, k * CK:k * CK + n], acc[:, k % 2, 0:n], ACT.Identity,
                                     bias=cb_col, scale=cw_col).then_inc(keys_copied, 1)

            act.wait_ge(pack_in, 16)
            act.wait_ge(pe_step, pe_did("h1"))
            nc.scalar.activation(h1_t, sc1[0:FO, :], ACT.Gelu_apprx_tanh, bias=b1_col[0:FO, :]).then_inc(act_step, 1)
            copy(x_t, sc0, "x_t")
            act.wait_ge(pe_step, pe_did("h2"))
            nc.scalar.activation(h2_t, pj[0:FO, :], ACT.Gelu_apprx_tanh, bias=b2_col[0:FO, :]).then_inc(act_step, 1)
            copy(v_time, tiles(sc0), "v")
            act.wait_ge(pe_step, pe_did("h3"))
            for j in range(LT):
                last = nc.scalar.activation(h_sb[:, j, :], tiles(sc1)[:, j, :], ACT.Copy, scale=decay[:, j:j + 1])
            last.then_inc(act_step, 1)
            act.wait_ge(pe_step, pe_did("u"))
            nc.scalar.activation(u_t, pj, ACT.Identity, bias=bu_col).then_inc(act_step, 1)
            for i, (to, f) in enumerate(((v_cos, 0), (v_cos, 1), (v_sin, 0), (v_sin, 1))):
                copy(to[:, f, :, :], scores[:, i // 2, i % 2, :].rearrange("p (b d) -> p b d", d=D), f"v_dft{i}")
            for i, (to, f) in enumerate(((h_cos, 0), (h_cos, 1), (h_sin, 0), (h_sin, 1))):
                bank = proj[:, i, :] if i < 2 else scores[:, (i - 2) // 2, (i - 2) % 2, :]
                copy(to[:, f, :, :], bank.rearrange("p (b d) -> p b d", d=D), f"h_dft{i}")
            for k in range(WHOLE + 1):
                turn_keys(k)

            def copy_weights(n):
                act.wait_ge(weights_in, n * 48)
                nc.scalar.activation(w_pair[:, :, :], w_next[:, :, :], ACT.Copy).then_inc(weights_copied, 1)

            copy_weights(1)
            for g in range(NH):
                act.wait_ge(lat_turned, g + 1)
                nc.scalar.activation(lat_t[:, g * HALF:(g + 1) * HALF], scores[:, 1, g, :], ACT.Identity,
                                     bias=lb_col, scale=lw_col).then_inc(lat_copied, 1)

            for i in range(2):
                nc.scalar.activation(scratch[:, i:i + 1], pack[:, 0:1], ACT.Exp).then_inc(exp_done, 1)

            def kv_copies(n, buf, width):
                act.wait_ge(proj_ready, n)
                dst = k_parts[:, buf, :, :] if buf < 2 else k_tail[:, :, :]
                for h in range(2):
                    r = slice(h * DH, (h + 1) * DH)
                    nc.scalar.activation(dst[r, h, 0:width], proj[r, 0, 0:width], ACT.Copy)
                vdst = v_sb[:, buf, :, :] if buf < 2 else v_tail[:, :, :]
                nc.scalar.activation(vdst, proj[:, 1, 0:width].rearrange("p (t n) -> p t n", n=P),
                                     ACT.Copy).then_inc(act_round, 1)

            def q_copy(n, h):
                act.wait_ge(proj_ready, n)
                nc.scalar.activation(q_parts[:, h, 0, :], q_bank[h], ACT.Copy).then_inc(act_round, 1)

            def exps(T, slot, rows=P):
                act.wait_ge(pv_done, T + 1)
                act.wait_ge(sum_done, T + 1)
                for n in range(NH):
                    act.wait_ge(scores_ready, T * 2 + n + 1)
                    nc.scalar.activation(probs[0:rows, slot, n, :, :], scores[0:rows, n, :, :], ACT.Exp,
                                         scale=SCALE).then_inc(exp_done, 1)

            def chunk(p, T, n, width=CK, buf=0):
                exps(T, 0)
                exps(T + 1, 1)
                kv_copies(n, buf, width)
                exps(T + 2, 2)
                exps(T + 3, 3)

            kv_copies(1, 0, CK)
            q_copy(2, 0)
            q_copy(3, 1)
            with act.Fori(0, pairs) as p:
                chunk(p, p * TILES, kv_round(p, 1), buf=1)
                with act.Fori(0, (WHOLE - 2) // 2) as i:
                    for b in range(2):
                        chunk(p, p * TILES + i * (2 * CT) + (b + 1) * CT, kv_round(p, i * 2 + b + 2), buf=b)
                chunk(p, p * TILES + (WHOLE - 1) * CT, kv_round(p, WHOLE), TAIL_K, 2)
                T = p * TILES + WHOLE * CT
                exps(T, 0)
                act.wait_ge(proj_ready, kv_round(p, WHOLE))
                copy_weights(p + 2)
                exps(T + 1, 1)
                kv_copies(p * ROUNDS + ROUNDS + 1, 0, CK)
                exps(T + 2, 2, SR)
                q_copy(p * ROUNDS + ROUNDS + 2, 0)
                q_copy(p * ROUNDS + ROUNDS + 3, 1)
                act.wait_ge(heads_done, p + 1)
                act.wait_ge(den_ready, p + 2)
                act.wait_ge(pv_done, p * TILES + TILES + PREV_SLOTS)
                nc.scalar.activation(den, pj, ACT.Copy)
                nc.scalar.activation(unscaled, acc[:, :, :], ACT.Copy).then_inc(pair_copied, 1)

            for g in range(NH):
                act.wait_ge(x2_turned, g + 1)
                nc.scalar.activation(x2_t[:, g * HALF:(g + 1) * HALF], scores[:, 1, g, :], ACT.Copy)\
                    .then_inc(x2_copied, 1)
            for g in range(NH):
                act.wait_ge(logits_ready, g + 1)
                nc.scalar.activation(logits[:, g * HT:(g + 1) * HT, :],
                                     proj[:, g, 0:HT * E].rearrange("p (j e) -> p j e", e=E), ACT.Copy)\
                    .then_inc(logits_copied, 1)
            for g in range(NH):
                act.wait_ge(gap_ready, g + 1)
                nc.scalar.activation(weight[:, 1, g * HT:(g + 1) * HT], weight[:, 0, g * HT:(g + 1) * HT], ACT.Exp)\
                    .then_inc(gap_exp, 1)

        @block.tensor
        def _(pe):
            mm, turn = nc.tensor.matmul, nc.tensor.transpose

            def turn_keys(k):
                pe.wait_ge(keys_normed, min((k * CT + CT - 1) // GC, ST // GC) + 1)
                if k >= 2:
                    pe.wait_ge(keys_copied, k - 1)
                for t in range(CT if k < WHOLE else TAIL_TILES):
                    j = k * CT + t
                    if j < ST:
                        last = turn(acc[:, k % 2, t * P:(t + 1) * P], keys_raw[:, j, :], ident)
                    else:
                        last = turn(acc[:, k % 2, t * P:t * P + SR], keys_last[:, :], ident[0:SR, 0:SR])
                last.then_inc(keys_turned, 1)

            def bias_row(view, row, j):
                mm(view, ones[0:1, :], row, start=True, stop=False)

            pe.wait_ge(filter_in, 32)
            for n in range(NH):
                last = mm(sc1[0:FO, n * HALF:(n + 1) * HALF], w_1, pe_t[:, n * HALF:(n + 1) * HALF],
                          start=True, stop=True)
            last.then_inc(pe_step, 1)
            pe.wait_ge(x_in, 16)
            pe.wait_ge(pack_in, 16)
            for j in range(LT):
                last = turn(sc0[:, j * P:(j + 1) * P], x_sb[:, j, :], ident)
            last.then_inc(pe_step, 1)
            pe.wait_ge(act_step, act_did("h1"))
            for n in range(NH):
                last = mm(pj[0:FO, n * HALF:(n + 1) * HALF], w_2, h1_t[:, n * HALF:(n + 1) * HALF],
                          start=True, stop=True)
            last.then_inc(pe_step, 1)
            pe.wait_ge(conv_w_in, 32)
            pe.wait_ge(ones_set, 1)
            pe.wait_ge(act_step, act_did("x_t"))
            for j in range(LT):
                bias_row(tiles(sc0)[:, j, :], b_v, j)
                last = mm(tiles(sc0)[:, j, :], x_t[:, j * P:(j + 1) * P], w_uvo[:, 1, :], start=False, stop=True)
            last.then_inc(pe_step, 1)
            pe.wait_ge(act_step, act_did("h2"))
            for j in range(LT):
                bias_row(tiles(sc1)[:, j, :], b_h, j)
                last = mm(tiles(sc1)[:, j, :], h2_t[:, j * P:(j + 1) * P], w_3, start=False, stop=True)
            last.then_inc(pe_step, 1)
            for n in range(NH):
                last = mm(pj[:, n * HALF:(n + 1) * HALF], w_uvo[:, 0, :], x_t[:, n * HALF:(n + 1) * HALF],
                          start=True, stop=True)
            last.then_inc(pe_step, 1)
            pe.wait_ge(dft_in, 32)
            pe.wait_ge(act_step, act_did("v"))
            spans = [slice(i * P, (i + 1) * P) for i in range(4)]
            v_blocks = v_time.rearrange("p (b w) d -> p w b d", w=2)
            h_blocks = h_sb.rearrange("p (b w) d -> p w b d", w=2)
            for i, f in enumerate(spans):
                if i == 2:
                    pe.wait_ge(act_step, act_did("h3"))
                bank = scores[:, i // 2, i % 2, :].rearrange("p (b d) -> p b d", d=D)
                mm(bank, fwd[:, 0, f], v_blocks[:, 0, :, :], start=True, stop=False)
                mm(bank, fwd[:, 1, f], v_blocks[:, 1, :, :], start=False, stop=True).then_inc(pe_step, 1)
            pe.wait_ge(act_step, act_did("u"))
            for i, f in enumerate(spans):
                if i >= 2:
                    pe.wait_ge(act_step, act_did(f"v_dft{i - 2}"))
                bank = (proj[:, i, :] if i < 2 else scores[:, (i - 2) // 2, (i - 2) % 2, :])
                bank = bank.rearrange("p (b d) -> p b d", d=D)
                mm(bank, fwd[:, 2, f], h_blocks[:, 0, :, :], start=True, stop=False)
                mm(bank[:, 1:NB, :], fwd[:, 0, f], h_blocks[:, 0, 0:NB - 1, :], start=False, stop=False)
                mm(bank[:, 1:NB, :], fwd[:, 1, f], h_blocks[:, 1, 0:NB - 1, :], start=False, stop=False)
                mm(bank, fwd[:, 3, f], h_blocks[:, 1, :, :], start=False, stop=True).then_inc(pe_step, 1)
            for k in range(WHOLE + 1):
                turn_keys(k)
            pe.wait_ge(act_step, act_did("h_dft3"))
            for b in range(NB):
                pe.wait_ge(spectrum_done, b + 1)
                for f in range(2 * 2):
                    y = (y_cos if f < 2 else y_sin)[:, f % 2, b, :]
                    last = mm(conv_bank[b], y, inv[:, f, :], start=(f == 0), stop=(f == 3))
                last.then_inc(conv_ready, 1)
            for g in range(NH):
                pe.wait_ge(y_done, 2 * g + 2)
                for j in range(g * HT, (g + 1) * HT):
                    bias_row(tiles(sc0)[:, j, :], b_o, j)
                    last = mm(tiles(sc0)[:, j, :], y_t[:, j * P:(j + 1) * P], w_uvo[:, 2, :], start=False, stop=True)
                last.then_inc(attn_ready, 1)

            def project_kv(n, src):
                pe.wait_ge(act_round, n - 1)
                pe.wait_ge(dve_round, n - 1)
                width = src.shape[1]
                mm(proj[:, 0, 0:width], w_pair[:, 0, :], src, start=True, stop=True)
                for t in range(width // P):
                    last = mm(proj[:, 1, t * P:(t + 1) * P], src[:, t * P:(t + 1) * P], w_pair[:, 1, :],
                              start=True, stop=True)
                last.then_inc(proj_ready, 1)

            def project_q(h):
                for m in range(NH):
                    last = mm(q_bank[h][:, m * HALF:(m + 1) * HALF], w_pair[:, 2 + h, :],
                              lat_t[:, m * HALF:(m + 1) * HALF], start=True, stop=True)
                last.then_inc(proj_ready, 1)

            def qk(T, k):
                for n in range(NH):
                    pe.wait_ge(exp_done, T * 2 + n + 1)
                    for h in range(2):
                        for part in range(2):
                            last = mm(scores[:, n, h, :], k[:, h, :], q_parts[:, h, part, n * HALF:(n + 1) * HALF],
                                      start=(part == 0), stop=(part == 1))
                    last.then_inc(scores_ready, 1)

            def pv(T, slot, v, first=False, final=False, rows=P):
                pe.wait_ge(clip_done, T + 1)
                for n in range(NH):
                    for h in range(2):
                        r = slice(h * DH, (h + 1) * DH)
                        last = mm(acc[r, n, :], v[0:rows, r], probs[0:rows, slot, n, h, :],
                                  start=first, stop=final)
                last.then_inc(pv_done, 1)

            def k_of(buf, t):
                return k_parts[:, buf, :, t * P:(t + 1) * P] if buf < 2 else k_tail[:, :, t * P:(t + 1) * P]

            def chunk(p, T, buf, n, src, stage_wait=None, opening=False):
                pe.wait_ge(act_round, n - 1)
                pe.wait_ge(dve_round, n - 1)
                for t in range(CT):
                    qk(T + t, k_of(buf, t))
                    if t >= LAG:
                        if opening and t == LAG:
                            pe.wait_ge(pair_copied, p + 1)
                        pv(T + (t - LAG), t - LAG, v_sb[:, buf, t - LAG, :], first=(opening and t == LAG))
                    elif not opening:
                        pv(T + t - LAG, CT - LAG + t, v_sb[:, 1 - buf, CT - LAG + t, :])
                    if t == 1:
                        if opening:
                            pe.wait_ge(pair_copied, p + 1)
                        if stage_wait is not None:
                            pe.wait_ge(*stage_wait)
                        project_kv(n, src)

            pe.wait_ge(pad_set, 1)
            pe.wait_ge(keys_copied, WHOLE + 1)
            pe.wait_ge(weights_copied, 1)
            mm(proj[:, 0, :], w_pair[:, 0, :], keys_t[:, 0:CK], start=True, stop=True)
            for t in range(CT):
                last = mm(proj[:, 1, t * P:(t + 1) * P], keys_t[:, t * P:(t + 1) * P], w_pair[:, 1, :],
                          start=True, stop=True)
            last.then_inc(proj_ready, 1)
            for g in range(NH):
                pe.wait_ge(lat_ready, g + 1)
                for j in range(g * HT, (g + 1) * HT):
                    last = turn(sc1[:, j * P:(j + 1) * P], lat[:, j, :], ident)
                last.then_inc(lat_turned, 1)
            pe.wait_ge(lat_copied, NH)
            pe.wait_ge(act_round, 1)
            pe.wait_ge(dve_round, 1)
            project_q(0)
            project_q(1)
            mm(acc[:, 0, 0:1], ident, ones[:, 0:1], start=True, stop=True).then_inc(pv_done, PREV_SLOTS)
            mm(acc[:, 0, 0:1], ident, ones[:, 0:1], start=True, stop=True).then_inc(den_ready, 1)
            with pe.Fori(0, pairs) as p:
                chunk(p, p * TILES, 0, kv_round(p, 1), keys_t[:, CK:2 * CK], opening=True)
                pairs_done = p * ((WHOLE - 2) // 2)
                with pe.Fori(0, (WHOLE - 2) // 2) as i:
                    for b in range(2):
                        chunk(p, p * TILES + i * (2 * CT) + (b + 1) * CT, 1 - b, kv_round(p, i * 2 + b + 2),
                              stage[:, b, :], stage_wait=(stage_in[b], (pairs_done + i) * 16 + 16))
                chunk(p, p * TILES + (WHOLE - 1) * CT, 1, kv_round(p, WHOLE), keys_t[:, WHOLE * CK:PADDED])
                T = p * TILES + WHOLE * CT
                pe.wait_ge(act_round, kv_round(p, WHOLE))
                pe.wait_ge(dve_round, kv_round(p, WHOLE))
                qk(T, k_of(2, 0))
                pv(T - 2, 2, v_sb[:, 1, 2, :])
                qk(T + 1, k_of(2, 1))
                pv(T - 1, 3, v_sb[:, 1, 3, :])
                pe.wait_ge(weights_copied, p + 2)
                project_kv(p * ROUNDS + ROUNDS + 1, keys_t[:, 0:CK])
                qk(T + 2, k_of(2, 2))
                pv(T, 0, v_tail[:, 0, :])
                pe.wait_ge(act_round, p * ROUNDS + ROUNDS + 1)
                pe.wait_ge(dve_round, p * ROUNDS + ROUNDS + 1)
                project_q(0)
                pe.wait_ge(exp_done, T * 2 + (2 * TAIL_TILES + 1))
                project_q(1)
                pv(T + 1, 1, v_tail[:, 1, :])
                pv(T + 2, 2, v_tail[:, 2, :], final=True, rows=SR)
                pe.wait_ge(act_round, p * ROUNDS + ROUNDS + 2)
                pe.wait_ge(dve_round, p * ROUNDS + ROUNDS + 2)
                pe.wait_ge(sum_done, p * TILES + TILES + PREV_SLOTS)
                for n in range(NH):
                    for h in range(2):
                        last = mm(proj[h * DH:(h + 1) * DH, n, :], ones[:, 0:DH], sums[:, n, h, :],
                                  start=True, stop=True)
                last.then_inc(den_ready, 1)

            pe.wait_ge(heads_done, pairs + 1)
            pe.wait_ge(act_round, pairs * ROUNDS + 3)
            pe.wait_ge(dve_round, pairs * ROUNDS + 3)
            pe.wait_ge(late_in, 48)
            for g in range(NH):
                for j in range(g * HT, (g + 1) * HT):
                    bias_row(tiles(sc0)[:, j, :], b_x, j)
                    for n in range(pairs):
                        last = mm(tiles(sc0)[:, j, :], heads_t[:, n, j * P:(j + 1) * P], w_xo[:, n, :],
                                  start=False, stop=(n == pairs - 1))
                last.then_inc(out_ready, 1)
            for g in range(NH):
                pe.wait_ge(x2_ready, g + 1)
                for j in range(g * HT, (g + 1) * HT):
                    last = turn(sc1[:, j * P:(j + 1) * P], x2[:, j, :], ident)
                last.then_inc(x2_turned, 1)
            for g in range(NH):
                pe.wait_ge(x2_copied, g + 1)
                for j in range(g * HT, (g + 1) * HT):
                    at = (j - g * HT) * E
                    last = mm(proj[:, g, at:at + E], x2_t[:, j * P:(j + 1) * P], w_router[:, :],
                              start=True, stop=True)
                last.then_inc(logits_ready, 1)

            experts = w_experts[:, :, :].rearrange("d e f -> d (e f)")
            pe.wait_ge(out_read, NH)

            def run_experts(j):
                if j >= 2:
                    pe.wait_ge(moe_added, j - 1)
                for n in range(2):
                    last = mm(scores[:, j % 2, n, :], x2_t[:, j * P:(j + 1) * P],
                              experts[:, n * HALF:(n + 1) * HALF], start=True, stop=True)
                last.then_inc(moe_ready, 1)

            run_experts(0)
            run_experts(1)
            for g in range(NH):
                pe.wait_ge(chosen_ready, g + 1)
                at, n = LT * E + g * HT * E, HT * E
                mm(acc[:, g, 0:n], earlier, chosen_pad[:, at:at + n], start=True, stop=False)
                for i in range(1, LT):
                    last = mm(acc[:, g, 0:n], ones[:, :], chosen_pad[:, at - i * E:at - i * E + n],
                              start=False, stop=(i == LT - 1))
                last.then_inc(places_ready, 1)
            for j in range(2, LT):
                run_experts(j)

        @block.vector
        def _(dve):
            v = nc.vector
            links = 0

            def link(ins):
                nonlocal links
                links += 1
                ins.then_inc(dve_link, 1)
                dve.wait_ge(dve_link, links)

            v.memset(ones[:, :], 1.0).then_inc(ones_set, 1)

            def key_statistics(g):
                dve.wait_ge(key_in[g], 16)
                for j in range(g * GC, (g + 1) * GC):
                    last = v.bn_stats(key_stat[:, j, :], keys_raw[:, j, :])
                link(last)
                for j in range(g * GC, (g + 1) * GC):
                    last = v.bn_aggr(key_mv[:, j, :], key_stat[:, j, :])
                last.then_inc(key_stats, 1)

            def key_norm(g):
                dve.wait_ge(key_stats, g + 1)
                dve.wait_ge(key_rstds, g + 1)
                for j in range(g * GC, (g + 1) * GC):
                    last = v.tensor_scalar(keys_raw[:, j, :], keys_raw[:, j, :], key_mv[:, j, 0:1],
                                           key_rstd[:, j:j + 1], ALU.subtract, ALU.mult)
                last.then_inc(keys_normed, 1)

            key_statistics(0)
            for g in range(1, ST // GC):
                key_statistics(g)
                key_norm(g - 1)
            key_norm(ST // GC - 1)
            dve.wait_ge(last_key_in, 16)
            link(v.bn_stats(key_stat[0:SR, ST, :], keys_last[:, :]))
            v.bn_aggr(key_mv[0:SR, ST, :], key_stat[0:SR, ST, :]).then_inc(key_stats, 1)
            dve.wait_ge(key_stats, ST // GC + 1)
            dve.wait_ge(key_rstds, ST // GC + 1)
            v.tensor_scalar(keys_last[:, :], keys_last[:, :], key_mv[0:SR, ST, 0:1], key_rstd[0:SR, ST:TILES],
                            ALU.subtract, ALU.mult).then_inc(keys_normed, 1)

            def gate_conv(b):
                dve.wait_ge(conv_ready, b + 1)
                v.tensor_tensor(y_t[:, b * BLK:(b + 1) * BLK], u_t[:, b * BLK:(b + 1) * BLK], conv_bank[b],
                                ALU.mult).then_inc(y_done, 1)

            dve.wait_ge(act_step, act_did("h_dft3"))
            link(v.tensor_copy(h_cos_n, h_cos))
            link(v.tensor_copy(h_cos_n[0:1, 0, :, :], h_sin[0:1, 0, :, :]))
            link(v.memset(h_sin[0:1, 0, :, :], 0.0))
            for d in range(NB):
                n = NB - d

                def window(t):
                    return t[:, :, d:d + 1, :].broadcast_to([P, 2, n, D])

                for to, first, second, op in ((y_cos, (v_cos, h_cos), (v_sin, h_sin), ALU.subtract),
                                              (y_sin, (v_cos, h_sin), (v_sin, h_cos_n), ALU.add)):
                    to = to[:, :, d:NB, :]
                    pa, pb = product_a[:, :, 0:n, :], product_b[:, :, 0:n, :]
                    v.tensor_tensor(pa if d else to, first[0][:, :, 0:n, :], window(first[1]), ALU.mult)
                    link(v.tensor_tensor(pb, second[0][:, :, 0:n, :], window(second[1]), ALU.mult))
                    if d:
                        link(v.tensor_tensor(to, to, pa, ALU.add))
                    last = v.tensor_tensor(to, to, pb, op)
                    if op == ALU.add:
                        last.then_inc(spectrum_done, 1)
                        if d < NB - 1:
                            dve.wait_ge(spectrum_done, d + 1)
                    else:
                        link(last)
                if d == NB - 2:
                    gate_conv(0)
                    gate_conv(1)

            def row_statistics(norm, g, frm):
                for j in range(g * HT, (g + 1) * HT):
                    last = v.bn_stats(row_stat[:, norm, j, :], frm[:, j, :])
                link(last)
                for j in range(g * HT, (g + 1) * HT):
                    last = v.bn_aggr(row_mv[:, norm, j, :], row_stat[:, norm, j, :])
                last.then_inc(row_stats, 1)

            def row_norm(norm, g, to, frm):
                dve.wait_ge(row_stats, norm * NH + g + 1)
                dve.wait_ge(row_rstds, norm * NH + g + 1)
                for j in range(g * HT, (g + 1) * HT):
                    last = v.tensor_scalar(to[:, j, :], frm[:, j, :], row_mv[:, norm, j, 0:1],
                                           row_rstd[:, norm, j:j + 1], ALU.subtract, ALU.mult)
                return last

            def add_rows(g, to, rows):
                half = slice(g * HT, (g + 1) * HT)
                return v.tensor_tensor(to[:, half, :], rows[:, half, :], tiles(sc0)[:, half, :], ALU.add)

            gate_conv(2)
            dve.wait_ge(attn_ready, 1)
            link(add_rows(0, resid, x_sb))
            row_statistics(0, 0, resid)
            gate_conv(3)
            dve.wait_ge(attn_ready, 2)
            link(add_rows(1, resid, x_sb))
            row_statistics(0, 1, resid)
            for g in range(NH):
                link(row_norm(0, g, x1, resid))
                row_statistics(1, g, x1)
            for g in range(NH):
                row_norm(1, g, lat, x1).then_inc(lat_ready, 1)
            v.memset(scratch[:, 4:5], 0.0).then_inc(sum_done, PREV_SLOTS)
            v.memset(unscaled, 0.0)
            v.memset(den, 1.0).then_inc(pair_copied, 1)

            def k_low(n, buf, width):
                dve.wait_ge(act_round, n)
                dst = k_parts[:, buf, :, :] if buf < 2 else k_tail[:, :, :]
                for h in range(2):
                    r, other = slice(h * DH, (h + 1) * DH), slice((1 - h) * DH, (2 - h) * DH)
                    last = v.tensor_tensor(dst[other, h, 0:width], proj[r, 0, 0:width],
                                           dst[r, h, 0:width].bitcast(F32), ALU.subtract)
                last.then_inc(dve_round, 1)

            def q_low(n, h):
                dve.wait_ge(act_round, n)
                v.tensor_tensor(q_parts[:, h, 1, :], q_bank[h], q_parts[:, h, 0, :].bitcast(F32), ALU.subtract)\
                    .then_inc(dve_round, 1)

            def clip(T, slot, rows=P):
                tile = probs[0:rows, slot, :, :, :]
                dve.wait_ge(exp_done, T * 2 + NH + 2)
                v.tensor_scalar(tile, tile, float(np.exp(CLIP)), float(np.exp(-CLIP)), ALU.min, ALU.max)\
                    .then_inc(clip_done, 1)

            def add_up(T, slot, rows=P, first=None):
                tile = probs[0:rows, slot, :, :, :]
                dve.wait_ge(clip_done, T + 1)
                dve.wait_ge(sum_done, T + PREV_SLOTS)
                if first is not None:
                    dve.wait_ge(den_ready, first + 1)
                    v.tensor_copy(sums[:, :, :, :], tile).then_inc(sum_done, 1)
                else:
                    v.tensor_tensor(sums[0:rows, :, :, :], sums[0:rows, :, :, :], tile, ALU.add)\
                        .then_inc(sum_done, 1)

            def chunk(p, T, n, width=CK, buf=0, opening=False):
                clip(T, 0)
                if not opening:
                    add_up(T - 1, CT - 1)
                clip(T + 1, 1)
                add_up(T, 0, first=p if opening else None)
                k_low(n, buf, width)
                clip(T + 2, 2)
                add_up(T + 1, 1)
                clip(T + 3, 3)
                add_up(T + 2, 2)

            k_low(1, 0, CK)
            q_low(2, 0)
            q_low(3, 1)
            PIECE = L // PIECES

            def invert(at):
                v.reciprocal(den[:, bass.ds(at, PIECE)], den[:, bass.ds(at, PIECE)]).then_inc(inverted, 1)

            def divide(p, to):
                dve.wait_ge(inverted, p * PIECES + PIECES)
                v.tensor_tensor(heads_flat[:, bass.ds(to * L, L)], unscaled.rearrange("p n q -> p (n q)"), den,
                                ALU.mult).then_inc(heads_done, 1)

            with dve.Fori(0, pairs) as p:
                chunk(p, p * TILES, kv_round(p, 1), buf=1, opening=True)
                dve.wait_ge(pair_copied, p + 1)
                invert(0)
                with dve.Fori(0, (WHOLE - 2) // 2) as i:
                    invert(i * PIECE + PIECE)
                    for b in range(2):
                        chunk(p, p * TILES + i * (2 * CT) + (b + 1) * CT, kv_round(p, i * 2 + b + 2), buf=b)
                invert((PIECES - 2) * PIECE)
                chunk(p, p * TILES + (WHOLE - 1) * CT, kv_round(p, WHOLE), TAIL_K, 2)
                invert((PIECES - 1) * PIECE)
                T = p * TILES + WHOLE * CT
                clip(T, 0)
                add_up(T - 1, CT - 1)
                clip(T + 1, 1)
                add_up(T, 0)
                k_low(p * ROUNDS + ROUNDS + 1, 0, CK)
                clip(T + 2, 2, SR)
                add_up(T + 1, 1)
                q_low(p * ROUNDS + ROUNDS + 2, 0)
                add_up(T + 2, 2, SR)
                q_low(p * ROUNDS + ROUNDS + 3, 1)
                divide(p, (p + (PAIRS - 1)) % PAIRS)

            dve.wait_ge(pair_copied, pairs + 1)
            for n in range(PIECES):
                invert(n * PIECE)
            divide(pairs, PAIRS - 1)

            for g in range(NH):
                dve.wait_ge(out_ready, g + 1)
                add_rows(g, moe, x1).then_inc(out_read, 1)
                dve.wait_ge(out_read, g + 1)
                row_statistics(2, g, moe)
            for g in range(NH):
                row_norm(2, g, x2, moe).then_inc(x2_ready, 1)
            v.memset(chosen_pad[:, 0:LT * E], 0.0)

            def per_tile(i, half):
                return weight[:, i, half].rearrange("p (j o) -> p j o", o=1).broadcast_to([P, HT, E])

            for g in range(NH):
                half = slice(g * HT, (g + 1) * HT)
                dve.wait_ge(logits_copied, g + 1)
                for j in range(g * HT, (g + 1) * HT):
                    last = v.max(top[:, j, :], logits[:, j, :])
                link(last)
                for j in range(g * HT, (g + 1) * HT):
                    last = v.max_index(top_at[:, j, :], top[:, j, :], logits[:, j, :])
                link(last)
                v.tensor_tensor(weight[:, 0, half], top[:, half, 1], top[:, half, 0], ALU.subtract).then_inc(gap_ready, 1)
                link(v.tensor_copy(top_no[:, half, :], top_at[:, half, :]))
                v.tensor_tensor(gate_one[:, half, :], expert_no[:, half, :],
                                top_no[:, half, 0:1].broadcast_to([P, HT, E]), ALU.is_equal)
                link(v.tensor_tensor(gate_two[:, half, :], expert_no[:, half, :],
                                     top_no[:, half, 1:2].broadcast_to([P, HT, E]), ALU.is_equal))
                v.tensor_tensor(chosen[:, half, :], gate_one[:, half, :], gate_two[:, half, :], ALU.add)\
                    .then_inc(chosen_ready, 1)
            for g in range(NH):
                half = slice(g * HT, (g + 1) * HT)
                one, two = gate_one[:, half, :], gate_two[:, half, :]
                dve.wait_ge(gap_exp, g + 1)
                link(v.tensor_scalar(weight[:, 2, half], weight[:, 1, half], 1.0, None, ALU.add))
                link(v.reciprocal(weight[:, 2, half], weight[:, 2, half]))
                link(v.tensor_tensor(weight[:, 3, half], weight[:, 1, half], weight[:, 2, half], ALU.mult))
                v.tensor_tensor(one, one, per_tile(2, half), ALU.mult)
                link(v.tensor_tensor(two, two, per_tile(3, half), ALU.mult))
                v.tensor_tensor(one, one, two, ALU.add)
                dve.wait_ge(places_ready, g + 1)
                link(v.tensor_scalar(kept[:, half, :], acc[:, g, 0:HT * E].rearrange("p (j e) -> p j e", e=E),
                                     float(CAP), None, ALU.is_lt))
                link(v.tensor_tensor(one, one, kept[:, half, :], ALU.mult))
            for j in range(LT):
                dve.wait_ge(moe_ready, j + 1)
                for e in range(E):
                    view = scores[:, j % 2, e // 4, (e % 4) * D:(e % 4 + 1) * D]
                    last = v.scalar_tensor_tensor(out=x3[:, j, :], in0=view, scalar=gate_one[:, j, e:e + 1],
                                                  in1=(x3 if e else x2)[:, j, :], op0=ALU.mult, op1=ALU.add)
                    if e < E - 1:
                        link(last)
                last.then_inc(moe_added, 1)
                if j % HT == HT - 1:
                    dve.wait_ge(moe_added, j + 1)
                    row_statistics(3, j // HT, x3)
            for g in range(NH):
                row_norm(3, g, moe, x3).then_inc(final_ready, 1)


_INS = ["x", "ctx_1024", "L0_xattn_Wq", "L0_xattn_Wkv", "L0_xattn_Wo", "L0_ffn_We"]


def kernel(**inputs):
    from concourse import bacc
    from concourse.bass_utils import run_bass_kernel_spmd

    arrays = {n: np.ascontiguousarray(inputs[n]) for n in _INS}
    arrays["router_t"] = np.ascontiguousarray(np.asarray(inputs["L0_ffn_Wr"]).T)
    arrays.update(constants())
    column = [inputs[n] for n in ("L0_attn_bu", "L0_attn_b1", "L0_attn_b2", "L0_xattn_ln_l_w", "L0_xattn_ln_l_b",
                                  "L0_xattn_ln_c_w", "L0_xattn_ln_c_b")]
    columns = np.zeros((P, len(column)), np.float32)
    for i, n in enumerate(column):
        columns[:n.shape[0], i] = n
    arrays["const_pack"] = np.concatenate([arrays.pop("c_pack"), columns], 1)
    arrays["filter_pack"] = np.concatenate([inputs["L0_attn_W1"], inputs["L0_attn_W2"], inputs["L0_attn_W3"]], 1)
    arrays["conv_pack"] = np.stack([inputs["L0_attn_Wu"], inputs["L0_attn_Wv"], inputs["L0_attn_Wo"]])
    arrays["row_pack"] = np.stack([inputs["L0_attn_bv"], inputs["L0_attn_b3"], inputs["L0_attn_bo"],
                                   inputs["L0_xattn_bo"]])
    nc = bacc.Bacc("TRN2", target_bir_lowering=False, num_devices=1)
    aps = {n: nc.dram_tensor(f"in_{n}", v.shape, mybir.dt.from_np(v.dtype), kind="ExternalInput").ap()
           for n, v in arrays.items()}
    out = nc.dram_tensor("out", (1, L, D), F32, kind="ExternalOutput").ap()
    build(nc, aps, out)
    r = run_bass_kernel_spmd(nc, [{f"in_{n}": v for n, v in arrays.items()}], core_ids=[0])
    return r.results[0]["out"]
```

```python
from contextlib import ExitStack

import numpy as np

import concourse.bass as bass
from concourse import mybir

F32 = mybir.dt.float32
F32R = mybir.dt.float32r
U32 = mybir.dt.uint32
ALU = mybir.AluOpType
ACT = mybir.ActivationFunctionType

P = 128
D = 128
L = 1024
LT = L // P
NH = 2
HT = LT // NH
HALF = L // NH
S = 6404
ST = S // P
SR = S - ST * P
TILES = ST + 1
H = 16
DH = 64
PAIRS = H // 2
CT = 4
CK = CT * P
WHOLE = ST // CT
TAIL_TILES = TILES - WHOLE * CT
TAIL_K = TAIL_TILES * P
PADDED = WHOLE * CK + TAIL_K
GC = 10
DVE_GROUPS = 3
E = 8
CAP = int(L * 2 / E * 1.5) + 1
FO = 64
BLK = 256
NB = L // BLK
W = 2 * BLK
CLIP = 11.0
EPS = 1e-5
SCALE = DH ** -0.5
ROUNDS = WHOLE + 1 + 2
INNER = (WHOLE - 2) // 2
PIECE = 64
PIECES = HALF // PIECE
FIRST_PIECES = PIECES - INNER
DEN_ROWS = 32
LAG = 2
PREV_SLOTS = 3


def constants():
    ident = np.eye(P)
    earlier = np.triu(np.ones((P, P)), 1)
    expert = np.tile(np.arange(E), (P, LT))
    t = np.arange(L)
    decay = np.exp(np.float32(-0.01) * t.astype(np.float32)).reshape(LT, P).T
    pack = np.concatenate([ident, earlier, expert, decay], 1).astype(np.float32)

    div = np.exp(np.arange(0, FO, 2, dtype=np.float32) * np.float32(-(np.log(10000.0) / FO)))
    ang = t.astype(np.float32)[:, None] * div.astype(np.float32)
    pe = np.zeros((L, FO), np.float32)
    pe[:, 0::2], pe[:, 1::2] = np.sin(ang), np.cos(ang)

    n, k = np.arange(W)[:, None], np.arange(BLK)[None, :]
    cos, sin = np.cos(2 * np.pi * n * k / W), np.sin(2 * np.pi * n * k / W)
    nyquist = np.cos(np.pi * n)
    sin_n = sin.copy()
    sin_n[:, :1] = nyquist
    forward = np.concatenate([cos, sin_n], 1)
    inv_cos = 2 * cos[BLK:].T / W
    inv_cos[0] /= 2
    inv_sin = 2 * sin[BLK:].T / W
    inv_sin[0] = nyquist[BLK:, 0] / W
    inverse = np.concatenate([inv_cos, inv_sin], 0)
    return {"c_pack": pack, "c_pe": np.ascontiguousarray(pe.T),
            "c_fwd": forward.astype(np.float32), "c_inv": inverse.astype(np.float32)}


def build(nc, a, out, pairs=PAIRS):
    ctx = ExitStack()
    with ctx:
        def sb(name, shape, dt=F32):
            return ctx.enter_context(nc.sbuf_tensor(name, shape, dt))

        def sem(name):
            return ctx.enter_context(nc.semaphore(name))

        pack = sb("pack", [P, 2 * P + LT * E + LT + 7])
        ident, earlier = pack[:, 0:P], pack[:, P:2 * P]
        expert_no = pack[:, 2 * P:2 * P + LT * E].rearrange("p (j e) -> p j e", e=E)
        decay = pack[:, 2 * P + LT * E:2 * P + LT * E + LT]
        bu_col, b1_col, b2_col, lw_col, lb_col, cw_col, cb_col = (
            pack[:, 2 * P + LT * E + LT + i:2 * P + LT * E + LT + i + 1] for i in range(7))
        ones = sb("ones", [P, P])
        bias_rows = sb("bias_rows", [P, 4, D])
        b_v, b_h, b_o, b_x = (bias_rows[:, i, :] for i in range(4))
        w_filter = sb("w_filter", [P, 2 * FO + D])
        w_1, w_2, w_3 = (w_filter[:, i:j] for i, j in ((0, FO), (FO, 2 * FO), (2 * FO, 2 * FO + D)))
        w_router = sb("w_router", [P, E])
        w_experts = sb("w_experts", [P, E, D])
        w_xo = sb("w_xo", [P, PAIRS, D])
        w_next = sb("w_next", [P, 4, P])
        w_pair = sb("w_pair", [P, 4, P])
        keys_t = sb("keys_t", [P, PADDED])
        stage = sb("stage", [P, 2, CK])
        k_parts = sb("k_parts", [P, 2, 2, CK], F32R)
        k_tail = sb("k_tail", [P, 2, TAIL_TILES * P], F32R)
        v_tail = sb("v_tail", [P, TAIL_TILES, P])
        q_parts = sb("q_parts", [P, 2, 2, L], F32R)
        lat_t = sb("lat_t", [P, L])
        probs = sb("probs", [P, CT, NH, 2, HALF])
        heads_t = sb("heads_t", [P, PAIRS, L])
        x1 = sb("x1", [P, LT, D])
        scratch = sb("scratch", [P, 8])

        products = sb("products", [P, 4, NB, D])

        keys_raw = sb("keys_raw", [P, ST, D])
        keys_last = sb("keys_last", [SR, D])

        def carve(t, at, shape):
            n = int(np.prod(shape[1:]))
            view = t[0:shape[0], at:at + n]
            if len(shape) == 3:
                view = view.rearrange("p (a b) -> p a b", b=shape[2])
            if len(shape) == 4:
                view = view.rearrange("p (a b c) -> p a b c", b=shape[2], c=shape[3])
            return view

        flat = probs[:, :, :, :, :].rearrange("p a b c d -> p (a b c d)")
        raw_flat = keys_raw[:, :, :].rearrange("p a b -> p (a b)")
        sums = carve(raw_flat, 2 * L, [P, NH, 2, HALF])
        unscaled = carve(raw_flat, 4 * L, [P, NH, HALF])
        den = carve(raw_flat, L, [P, HALF])
        inverses = carve(raw_flat, 0, [P, NH, HALF])
        v_sb = carve(raw_flat, 5 * L, [P, 2, CT, P])
        heads_flat = heads_t[:, :, :].rearrange("p a b -> p (a b)")
        x_t = carve(heads_flat, 0, [P, L])
        h1_t = carve(heads_flat, L, [P, L])
        h2_t = carve(heads_flat, 2 * L, [P, L])
        h_sb = carve(heads_flat, 3 * L, [P, LT, D])
        v_time = carve(heads_flat, 4 * L, [P, LT, D])
        u_t = carve(heads_flat, 5 * L, [P, L])
        inv = carve(heads_flat, 7 * L, [P, W // P, BLK])
        y_cos = carve(heads_flat, 0, [P, 2, NB, D])
        y_sin = carve(heads_flat, L, [P, 2, NB, D])
        y_t = carve(heads_flat, 3 * L, [P, L])
        v_cos = carve(flat, 0, [P, 2, NB, D])
        v_sin = carve(flat, L, [P, 2, NB, D])
        h_cos = carve(flat, 2 * L, [P, 2, NB, D])
        h_sin = carve(flat, 3 * L, [P, 2, NB, D])
        h_cos_n = carve(flat, 4 * L, [P, NB, D])
        fwd = carve(flat, 5 * L, [P, W // P, 2 * BLK])
        x_sb = carve(flat, 7 * L, [P, LT, D])
        w_uvo = v_tail
        pe_t = x1[:, :, :].rearrange("p a b -> p (a b)")
        resid = carve(flat, 0, [P, LT, D])
        lat = carve(raw_flat, L, [P, LT, D])

        key_stat = sb("key_stat", [P, TILES, 6])
        key_mv = sb("key_mv", [P, TILES, 2])
        key_rstd = sb("key_rstd", [P, TILES])
        key_shift = sb("key_shift", [P, TILES])
        half_neg = sb("half_neg", [P, TILES])
        row_stat = sb("row_stat", [P, 4, LT, 6])
        row_mv = sb("row_mv", [P, 4, LT, 2])
        row_rstd = sb("row_rstd", [P, 4, LT])

        x2 = carve(flat, 0, [P, LT, D])
        x2_t = carve(flat, L, [P, L])
        x3 = carve(flat, 2 * L, [P, LT, D])
        moe = carve(flat, 3 * L, [P, LT, D])
        small = carve(flat, 4 * L, [P, 5 * LT * E])
        odd = carve(flat, 7 * L, [P, 4, D])
        gate_one, gate_two, kept, chosen = (small[:, i * LT * E:(i + 1) * LT * E].rearrange("p (j e) -> p j e", e=E)
                                            for i in (0, 1, 2, 4))
        chosen_pad = small[:, 3 * LT * E:5 * LT * E]
        before = carve(flat, 6 * L, [P, 3, 2 * LT * E])
        logits, top, top_no = (carve(flat, 5 * L + i * LT * E, [P, LT, E]) for i in range(3))
        top_at = sb("top_at", [P, LT, E], U32)
        weight = carve(flat, 5 * L + 3 * LT * E, [P, 4, LT])

        scores = ctx.enter_context(nc.psum_tensor("scores", [P, NH, 2, HALF], F32))
        acc = ctx.enter_context(nc.psum_tensor("acc", [P, NH, HALF], F32))
        proj = ctx.enter_context(nc.psum_tensor("proj", [P, 2, HALF], F32))
        sc0 = scores[:, 0, :, :].rearrange("p b n -> p (b n)")
        sc1 = scores[:, 1, :, :].rearrange("p b n -> p (b n)")
        pj = proj[:, :, :].rearrange("p b n -> p (b n)")
        q_bank = [pj, sc0]
        expert_banks = [scores[:, :, 0, :], acc, scores[:, :, 1, :], proj]
        places = [proj[:, 1, :], acc[:, 0, :]]
        conv_bank = [bank[:, 0:BLK] for bank in (proj[:, 0, :], proj[:, 1, :], scores[:, 1, 0, :], scores[:, 1, 1, :])]
        h_bank = [[proj[:, 0, :], proj[:, 1, :]], [scores[:, 0, 0, :], scores[:, 0, 1, :]]]

        def tiles(view):
            return view.rearrange("p (j d) -> p j d", d=D)

        x_in, pack_in, filter_in, conv_w_in, dft_in, late_in = (
            sem(n) for n in ("x_in", "pack_in", "filter_in", "conv_w_in", "dft_in", "late_in"))
        key_in = [sem(f"key_in{g}") for g in range(ST // GC)]
        last_key_in = sem("last_key_in")
        ones_set = sem("ones_set")
        key_stats, key_rstds = sem("key_stats"), sem("key_rstds")
        keys_normed, keys_normed_act = sem("keys_normed"), sem("keys_normed_act")
        keys_turned, keys_copied = sem("keys_turned"), sem("keys_copied")
        pad_set, bias_pad_set, filter_pad_set = sem("pad_set"), sem("bias_pad_set"), sem("filter_pad_set")
        pe_step, act_step = sem("pe_step"), sem("act_step")
        dve_link, pool_link = sem("dve_link"), sem("pool_link")
        row_stats, row_rstds = sem("row_stats"), sem("row_rstds")
        weights_in, weights_copied = sem("weights_in"), sem("weights_copied")
        stage_in = [sem("stage_in0"), sem("stage_in1")]
        proj_ready, act_round, dve_round = sem("proj_ready"), sem("act_round"), sem("dve_round")
        den_ready, den_copied, inverted, inverses_ready = (
            sem(n) for n in ("den_ready", "den_copied", "inverted", "inverses_ready"))
        acc_copied, heads_done = sem("acc_copied"), sem("heads_done")
        half_spectrum_done, spectrum_done = sem("half_spectrum_done"), sem("spectrum_done")
        conv_ready, y_done = sem("conv_ready"), sem("y_done")
        attn_ready, lat_ready, lat_turned, lat_copied = (
            sem(n) for n in ("attn_ready", "lat_ready", "lat_turned", "lat_copied"))
        scores_ready, exp_done, clip_done = sem("scores_ready"), sem("exp_done"), sem("clip_done")
        sum_done, pv_done = sem("sum_done"), sem("pv_done")
        out_ready, x2_ready, x2_turned, x2_copied, logits_ready, logits_copied = (
            sem(n) for n in ("out_ready", "x2_ready", "x2_turned", "x2_copied", "logits_ready", "logits_copied"))
        out_read, gap_ready, gap_exp, chosen_ready, places_ready, places_read, final_ready = (
            sem(n) for n in ("out_read", "gap_ready", "gap_exp", "chosen_ready", "places_ready", "places_read",
                             "final_ready"))
        moe_ready, moe_added = sem("moe_ready"), sem("moe_added")
        stored = sem("stored")

        STEPS = ["h1", "x_t", "h2", "v", "h3", "u", "v_cos0", "v_sin0", "h_cos0", "h_sin0",
                 "v_cos1", "v_sin1", "h_cos1", "h_sin1"]

        NORMS = [(0, 0), (0, 1), (1, 0), (1, 1), (2, 0), (2, 1), (3, 0), (3, 1)]

        def did(name):
            return STEPS.index(name) + 1

        def kv_round(p, c):
            return p * ROUNDS + c + 3

        block = ctx.enter_context(nc.Block())

        @block.sync
        def _(sp):
            sp.dma_start(x_sb[:, :, :], a["x"].rearrange("b (j p) d -> p (b j) d", p=P)).then_inc(x_in, 16)
            keys = a["ctx_1024"][0, 0:ST * P, :].rearrange("(p j) d -> p j d", j=ST)
            for g in range(ST // GC):
                sp.dma_start(keys_raw[:, g * GC:(g + 1) * GC, :], keys[:, g * GC:(g + 1) * GC, :])\
                    .then_inc(key_in[g], 16)
            sp.dma_start(keys_last[:, :], a["ctx_1024"][0, ST * P:S, :]).then_inc(last_key_in, 16)

            wkv = a["L0_xattn_Wkv"].rearrange("d (two n) -> d two n", two=2)

            def load_weights(p):
                sp.dma_start(w_next[:, 0:2, :], wkv[:, :, bass.ds(p * P, P)]).then_inc(weights_in, 16)
                for copy in range(2):
                    wq = a["L0_xattn_Wq"][:, bass.ds(p * P, P)].rearrange("d (h n) -> d h n", h=2)
                    sp.dma_start(w_next[:, 2:4, copy * DH:(copy + 1) * DH], wq).then_inc(weights_in, 16)

            load_weights(0)
            sp.dma_start(w_experts[:, :, :], a["L0_ffn_We"].rearrange("e d f -> d e f")).then_inc(late_in, 16)
            sp.dma_start(w_xo[:, :, :], a["L0_xattn_Wo"].rearrange("(g p) d -> p g d", p=P)).then_inc(late_in, 16)
            sp.dma_start(w_router[:, :], a["router_t"]).then_inc(late_in, 16)
            sp.wait_ge(keys_copied, WHOLE + 1)
            with sp.Fori(0, pairs) as p:
                sp.wait_ge(weights_copied, p + 1)
                load_weights((p + 1) % pairs)
                with sp.Fori(0, INNER) as i:
                    for b in range(2):
                        sp.wait_ge(proj_ready, kv_round(p, i * 2 + b))
                        sp.dma_start(stage[:, b, :], keys_t[:, bass.ds(i * (2 * CK) + (b + 2) * CK, CK)])\
                            .then_inc(stage_in[b], 16)
            for g in range(NH):
                sp.wait_ge(final_ready, g + 1)
                sp.dma_start(out[0, g * HALF:(g + 1) * HALF, :].rearrange("(j p) d -> p j d", p=P),
                             moe[:, g * HT:(g + 1) * HT, :]).then_inc(stored, 16)
            sp.wait_ge(stored, 32)

        @block.gpsimd
        def _(pool):
            pool.memset(bias_rows[:, :, :], 0.0).then_inc(bias_pad_set, 1)
            pool.wait_ge(bias_pad_set, 1)
            pool.memset(heads_flat[FO:P, L:3 * L], 0.0).then_inc(filter_pad_set, 1)
            pool.wait_ge(filter_pad_set, 1)
            pool.memset(half_neg[:, :], -0.5)
            pool.memset(keys_t[:, S:PADDED], 0.0).then_inc(pad_set, 1)
            links = 0

            def rstd(to, mv):
                nonlocal links
                pool.tensor_scalar(to, mv, EPS, None, ALU.add).then_inc(pool_link, 1)
                links += 1
                pool.wait_ge(pool_link, links)
                return pool.tensor_tensor(to, to, half_neg[0:to.shape[0], 0:to.shape[1]], ALU.pow)

            pool.wait_ge(pad_set, 1)
            for g in range(ST // GC):
                pool.wait_ge(key_stats, g + 1)
                span = slice(g * GC, (g + 1) * GC)
                last = rstd(key_rstd[:, span], key_mv[:, span, 1])
                if g >= DVE_GROUPS:
                    last.then_inc(pool_link, 1)
                    links += 1
                    pool.wait_ge(pool_link, links)
                    pool.tensor_tensor(key_shift[:, span], key_mv[:, span, 0], key_rstd[:, span], ALU.mult)\
                        .then_inc(pool_link, 1)
                    links += 1
                    pool.wait_ge(pool_link, links)
                    last = pool.tensor_scalar(key_shift[:, span], key_shift[:, span], -1.0, None, ALU.mult)
                last.then_inc(key_rstds, 1)
            pool.wait_ge(key_stats, ST // GC + 1)
            rstd(key_rstd[0:SR, ST:TILES], key_mv[0:SR, ST:TILES, 1]).then_inc(key_rstds, 1)
            pool.wait_ge(keys_copied, WHOLE + 1)
            pool.memset(sums, 1.0).then_inc(sum_done, PREV_SLOTS)
            pool.memset(unscaled, 0.0).then_inc(acc_copied, 1)
            for n, (norm, g) in enumerate(NORMS):
                span = slice(g * HT, (g + 1) * HT)
                pool.wait_ge(row_stats, n + 1)
                rstd(row_rstd[:, norm, span], row_mv[:, norm, span, 1]).then_inc(row_rstds, 1)

        @block.scalar
        def _(act):
            act.dma_start(pe_t, a["c_pe"]).then_inc(filter_in, 16)
            act.dma_start(w_filter[:, :], a["filter_pack"]).then_inc(filter_in, 16)
            act.dma_start(pack[:, :], a["const_pack"]).then_inc(pack_in, 16)
            act.dma_start(w_uvo[:, :, :], a["conv_pack"].rearrange("n d e -> d n e")).then_inc(conv_w_in, 16)
            act.wait_ge(bias_pad_set, 1)
            act.dma_start(bias_rows[0:1, :, :], a["row_pack"].rearrange("(o n) d -> o n d", o=1)).then_inc(conv_w_in, 16)
            act.dma_start(fwd[:, :, :], a["c_fwd"].rearrange("(w p) k -> p w k", p=P)).then_inc(dft_in, 16)
            act.dma_start(inv[:, :, :], a["c_inv"].rearrange("(w p) k -> p w k", p=P)).then_inc(dft_in, 16)

            def copy(to, frm, step):
                act.wait_ge(pe_step, did(step))
                nc.scalar.activation(to, frm, ACT.Copy).then_inc(act_step, 1)

            def turn_keys(k):
                n = CK if k < WHOLE else S - WHOLE * CK
                act.wait_ge(keys_turned, k + 1)
                nc.scalar.activation(keys_t[:, k * CK:k * CK + n], acc[:, k % 2, 0:n], ACT.Identity,
                                     bias=cb_col, scale=cw_col).then_inc(keys_copied, 1)

            act.wait_ge(pack_in, 16)
            act.wait_ge(pe_step, did("h1"))
            nc.scalar.activation(h1_t[0:FO, :], sc1[0:FO, :], ACT.Gelu_apprx_tanh, bias=b1_col[0:FO, :]).then_inc(act_step, 1)
            copy(x_t, sc0, "x_t")
            act.wait_ge(pe_step, did("h2"))
            nc.scalar.activation(h2_t[0:FO, :], pj[0:FO, :], ACT.Gelu_apprx_tanh, bias=b2_col[0:FO, :]).then_inc(act_step, 1)
            copy(v_time, tiles(sc0), "v")
            act.wait_ge(pe_step, did("h3"))
            for j in range(LT):
                last = nc.scalar.activation(h_sb[:, j, :], tiles(sc1)[:, j, :], ACT.Copy, scale=decay[:, j:j + 1])
            last.then_inc(act_step, 1)
            act.wait_ge(pe_step, did("u"))
            nc.scalar.activation(u_t, pj, ACT.Identity, bias=bu_col).then_inc(act_step, 1)
            for f in range(2):
                for to, bank, step in ((v_cos, scores[:, f, 0, :], "v_cos"), (v_sin, scores[:, f, 1, :], "v_sin"),
                                       (h_cos, h_bank[f][0], "h_cos"), (h_sin, h_bank[f][1], "h_sin")):
                    copy(to[:, f, :, :], bank.rearrange("p (b d) -> p b d", d=D), f"{step}{f}")
                g = DVE_GROUPS + f
                act.wait_ge(key_rstds, g + 1)
                for j in range(g * GC, (g + 1) * GC):
                    last = nc.scalar.activation(keys_raw[:, j, :], keys_raw[:, j, :], ACT.Identity,
                                                bias=key_shift[:, j:j + 1], scale=key_rstd[:, j:j + 1])
                last.then_inc(keys_normed_act, 1)
            for k in range(WHOLE + 1):
                turn_keys(k)

            def copy_weights(n):
                act.wait_ge(weights_in, n * 48)
                nc.scalar.activation(w_pair[:, :, :], w_next[:, :, :], ACT.Copy).then_inc(weights_copied, 1)

            copy_weights(1)
            for i in range(2):
                nc.scalar.activation(scratch[:, i:i + 1], pack[:, 0:1], ACT.Exp).then_inc(exp_done, 1)

            def kv_copies(n, buf, width):
                act.wait_ge(proj_ready, n)
                dst = k_parts[:, buf, :, :] if buf < 2 else k_tail[:, :, :]
                for h in range(2):
                    r = slice(h * DH, (h + 1) * DH)
                    nc.scalar.activation(dst[r, h, 0:width], proj[r, 0, 0:width], ACT.Copy)
                vdst = v_sb[:, buf, :, :] if buf < 2 else v_tail[:, :, :]
                nc.scalar.activation(vdst, proj[:, 1, 0:width].rearrange("p (t n) -> p t n", n=P),
                                     ACT.Copy).then_inc(act_round, 1)

            def q_copy(n, h):
                act.wait_ge(proj_ready, n)
                nc.scalar.activation(q_parts[:, h, 0, :], q_bank[h], ACT.Copy).then_inc(act_round, 1)

            def exps(T, slot):
                act.wait_ge(pv_done, T + 1)
                act.wait_ge(sum_done, T + 1)
                for n in range(NH):
                    act.wait_ge(scores_ready, T * 2 + n + 1)
                    nc.scalar.activation(probs[:, slot, n, :, :], scores[:, n, :, :], ACT.Exp,
                                         scale=SCALE).then_inc(exp_done, 1)

            def copy_den(n):
                act.wait_ge(den_ready, n)
                nc.scalar.activation(den, proj[:, 0, :], ACT.Copy).then_inc(den_copied, 1)

            def spread_inverses(m):
                for h in range(2):
                    frm = den[(2 * h + m) * DEN_ROWS:(2 * h + m + 1) * DEN_ROWS, :]
                    for at in range(h * DH, (h + 1) * DH, DEN_ROWS):
                        last = nc.scalar.activation(inverses[at:at + DEN_ROWS, m, :], frm, ACT.Copy)
                return last

            def chunk(p, T, n, width=CK, buf=0, opening=False):
                exps(T, 0)
                if opening:
                    copy_den(p + 1)
                exps(T + 1, 1)
                kv_copies(n, buf, width)
                exps(T + 2, 2)
                exps(T + 3, 3)

            kv_copies(1, 0, CK)
            for g in range(NH):
                act.wait_ge(lat_turned, g + 1)
                nc.scalar.activation(lat_t[:, g * HALF:(g + 1) * HALF], acc[:, g, :], ACT.Identity,
                                     bias=lb_col, scale=lw_col).then_inc(lat_copied, 1)
                act.wait_ge(proj_ready, g + 2)
                for h in range(2):
                    last = nc.scalar.activation(q_parts[:, h, 0, g * HALF:(g + 1) * HALF],
                                                q_bank[h][:, g * HALF:(g + 1) * HALF], ACT.Copy)
                last.then_inc(act_round, 1)
            with act.Fori(0, pairs) as p:
                chunk(p, p * TILES, kv_round(p, 1), buf=1, opening=True)
                with act.Fori(0, INNER) as i:
                    for b in range(2):
                        chunk(p, p * TILES + i * (2 * CT) + (b + 1) * CT, kv_round(p, i * 2 + b + 2), buf=b)
                act.wait_ge(inverted, p * PIECES + PIECES)
                spread_inverses(0)
                spread_inverses(1).then_inc(inverses_ready, 1)
                chunk(p, p * TILES + (WHOLE - 1) * CT, kv_round(p, WHOLE), TAIL_K, 2)
                T = p * TILES + WHOLE * CT
                exps(T, 0)
                act.wait_ge(proj_ready, kv_round(p, WHOLE))
                copy_weights(p + 2)
                exps(T + 1, 1)
                kv_copies(p * ROUNDS + ROUNDS + 1, 0, CK)
                exps(T + 2, 2)
                q_copy(p * ROUNDS + ROUNDS + 2, 0)
                q_copy(p * ROUNDS + ROUNDS + 3, 1)
                act.wait_ge(heads_done, p + 1)
                act.wait_ge(pv_done, p * TILES + TILES + PREV_SLOTS)
                nc.scalar.activation(unscaled, acc[:, :, :], ACT.Copy).then_inc(acc_copied, 1)
            copy_den(pairs + 1)
            act.wait_ge(inverted, (pairs + 1) * PIECES)
            for m in range(NH):
                spread_inverses(m).then_inc(inverses_ready, 1)

            for g in range(NH):
                half = slice(g * HT, (g + 1) * HT)
                act.wait_ge(x2_turned, g + 1)
                nc.scalar.activation(x2_t[:, g * HALF:(g + 1) * HALF], scores[:, 1, g, :], ACT.Copy)\
                    .then_inc(x2_copied, 1)
                act.wait_ge(logits_ready, g + 1)
                nc.scalar.activation(logits[:, half, :],
                                     proj[:, 0, g * HT * E:(g + 1) * HT * E].rearrange("p (j e) -> p j e", e=E),
                                     ACT.Copy).then_inc(logits_copied, 1)
                act.wait_ge(gap_ready, g + 1)
                nc.scalar.activation(weight[:, 1, half], weight[:, 0, half], ACT.Exp).then_inc(gap_exp, 1)

        @block.tensor
        def _(pe):
            mm, turn = nc.tensor.matmul, nc.tensor.transpose

            def turn_keys(k):
                g = min(k * CT + CT - 1, ST - 1) // GC
                if g < DVE_GROUPS:
                    pe.wait_ge(keys_normed, g + 1)
                else:
                    pe.wait_ge(keys_normed_act, g - DVE_GROUPS + 1)
                if k == WHOLE:
                    pe.wait_ge(keys_normed, DVE_GROUPS + 1)
                if k >= 2:
                    pe.wait_ge(keys_copied, k - 1)
                for t in range(CT if k < WHOLE else TAIL_TILES):
                    j = k * CT + t
                    if j < ST:
                        last = turn(acc[:, k % 2, t * P:(t + 1) * P], keys_raw[:, j, :], ident)
                    else:
                        last = turn(acc[:, k % 2, t * P:t * P + SR], keys_last[:, :], ident[0:SR, 0:SR])
                last.then_inc(keys_turned, 1)

            def bias_row(view, row, start=True):
                mm(view, ones[:, :], row, start=start, stop=False)

            pe.wait_ge(filter_in, 32)
            for n in range(NH):
                last = mm(sc1[0:FO, n * HALF:(n + 1) * HALF], w_1, pe_t[:, n * HALF:(n + 1) * HALF],
                          start=True, stop=True)
            last.then_inc(pe_step, 1)
            pe.wait_ge(x_in, 16)
            pe.wait_ge(pack_in, 16)
            for j in range(LT):
                last = turn(sc0[:, j * P:(j + 1) * P], x_sb[:, j, :], ident)
            last.then_inc(pe_step, 1)
            pe.wait_ge(filter_pad_set, 1)
            pe.wait_ge(act_step, did("h1"))
            for n in range(NH):
                last = mm(pj[0:FO, n * HALF:(n + 1) * HALF], w_2, h1_t[:, n * HALF:(n + 1) * HALF],
                          start=True, stop=True)
            last.then_inc(pe_step, 1)
            pe.wait_ge(conv_w_in, 32)
            pe.wait_ge(ones_set, 1)
            pe.wait_ge(act_step, did("x_t"))
            for j in range(LT):
                bias_row(tiles(sc0)[:, j, :], b_v)
                last = mm(tiles(sc0)[:, j, :], x_t[:, j * P:(j + 1) * P], w_uvo[:, 1, :], start=False, stop=True)
            last.then_inc(pe_step, 1)
            pe.wait_ge(act_step, did("h2"))
            for j in range(LT):
                bias_row(tiles(sc1)[:, j, :], b_h)
                last = mm(tiles(sc1)[:, j, :], h2_t[:, j * P:(j + 1) * P], w_3, start=False, stop=True)
            last.then_inc(pe_step, 1)
            for n in range(NH):
                last = mm(pj[:, n * HALF:(n + 1) * HALF], w_uvo[:, 0, :], x_t[:, n * HALF:(n + 1) * HALF],
                          start=True, stop=True)
            last.then_inc(pe_step, 1)
            pe.wait_ge(dft_in, 32)
            pe.wait_ge(act_step, did("v"))
            v_blocks = v_time.rearrange("p (b w) d -> p w b d", w=2)
            h_blocks = h_sb.rearrange("p (b w) d -> p w b d", w=2)
            for f in range(2):
                if f == 1:
                    pe.wait_ge(act_step, did("h3"))
                for i in range(2):
                    span = slice((2 * i + f) * P, (2 * i + f + 1) * P)
                    bank = scores[:, f, i, :].rearrange("p (b d) -> p b d", d=D)
                    mm(bank, fwd[:, 0, span], v_blocks[:, 0, :, :], start=True, stop=False)
                    mm(bank, fwd[:, 1, span], v_blocks[:, 1, :, :], start=False, stop=True).then_inc(pe_step, 1)
                pe.wait_ge(act_step, did("v_sin0" if f else "u"))
                for i in range(2):
                    span = slice((2 * i + f) * P, (2 * i + f + 1) * P)
                    bank = h_bank[f][i].rearrange("p (b d) -> p b d", d=D)
                    mm(bank, fwd[:, 2, span], h_blocks[:, 0, :, :], start=True, stop=False)
                    mm(bank[:, 1:NB, :], fwd[:, 0, span], h_blocks[:, 0, 0:NB - 1, :], start=False, stop=False)
                    mm(bank[:, 1:NB, :], fwd[:, 1, span], h_blocks[:, 1, 0:NB - 1, :], start=False, stop=False)
                    mm(bank, fwd[:, 3, span], h_blocks[:, 1, :, :], start=False, stop=True).then_inc(pe_step, 1)
            for k in range(WHOLE + 1):
                turn_keys(k)
            pe.wait_ge(act_step, did("h_sin1"))
            pe.wait_ge(half_spectrum_done, 1)
            for b in range(NB):
                mm(conv_bank[b], y_cos[:, 0, b, :], inv[:, 0, :], start=True, stop=False)
                mm(conv_bank[b], y_sin[:, 0, b, :], inv[:, 2, :], start=False, stop=False)

            def finish_conv(b):
                pe.wait_ge(spectrum_done, b + 1)
                mm(conv_bank[b], y_cos[:, 1, b, :], inv[:, 1, :], start=False, stop=False)
                mm(conv_bank[b], y_sin[:, 1, b, :], inv[:, 3, :], start=False, stop=True).then_inc(conv_ready, 1)

            def conv_output(g):
                pe.wait_ge(y_done, 2 * g + 2)
                for j in range(g * HT, (g + 1) * HT):
                    bias_row(tiles(sc0)[:, j, :], b_o)
                    last = mm(tiles(sc0)[:, j, :], y_t[:, j * P:(j + 1) * P], w_uvo[:, 2, :], start=False, stop=True)
                last.then_inc(attn_ready, 1)

            def turn_lat(g):
                pe.wait_ge(lat_ready, g + 1)
                for j in range(HT):
                    last = turn(acc[:, g, j * P:(j + 1) * P], lat[:, g * HT + j, :], ident)
                last.then_inc(lat_turned, 1)

            def first_q(g):
                half = slice(g * HALF, (g + 1) * HALF)
                pe.wait_ge(lat_copied, g + 1)
                for h in range(2):
                    last = mm(q_bank[h][:, half], w_pair[:, 2 + h, :], lat_t[:, half], start=True, stop=True)
                last.then_inc(proj_ready, 1)

            for b in range(NB):
                finish_conv(b)
            for g in range(NH):
                conv_output(g)
            pe.wait_ge(pad_set, 1)
            pe.wait_ge(keys_copied, WHOLE + 1)
            pe.wait_ge(weights_copied, 1)
            mm(proj[:, 0, :], w_pair[:, 0, :], keys_t[:, 0:CK], start=True, stop=True)
            for t in range(CT):
                last = mm(proj[:, 1, t * P:(t + 1) * P], keys_t[:, t * P:(t + 1) * P], w_pair[:, 1, :],
                          start=True, stop=True)
            last.then_inc(proj_ready, 1)
            turn_lat(0)
            pe.wait_ge(act_round, 1)
            pe.wait_ge(dve_round, 1)
            first_q(0)
            turn_lat(1)
            first_q(1)

            def project_kv(n, src):
                pe.wait_ge(act_round, n - 1)
                pe.wait_ge(dve_round, n - 1)
                width = src.shape[1]
                mm(proj[:, 0, 0:width], w_pair[:, 0, :], src, start=True, stop=True)
                for t in range(width // P):
                    last = mm(proj[:, 1, t * P:(t + 1) * P], src[:, t * P:(t + 1) * P], w_pair[:, 1, :],
                              start=True, stop=True)
                last.then_inc(proj_ready, 1)

            def project_q(h):
                for m in range(NH):
                    last = mm(q_bank[h][:, m * HALF:(m + 1) * HALF], w_pair[:, 2 + h, :],
                              lat_t[:, m * HALF:(m + 1) * HALF], start=True, stop=True)
                last.then_inc(proj_ready, 1)

            def qk(T, k):
                for n in range(NH):
                    pe.wait_ge(exp_done, T * 2 + n + 1)
                    for h in range(2):
                        for part in range(2):
                            last = mm(scores[:, n, h, :], k[:, h, :], q_parts[:, h, part, n * HALF:(n + 1) * HALF],
                                      start=(part == 0), stop=(part == 1))
                    last.then_inc(scores_ready, 1)

            def pv(T, slot, v, first=False, final=False):
                pe.wait_ge(clip_done, T + 1)
                for n, h in ((0, 0), (0, 1), (1, 1), (1, 0)):
                    r = slice(h * DH, (h + 1) * DH)
                    last = mm(acc[r, n, :], v[:, r], probs[:, slot, n, h, :], start=first, stop=final)
                last.then_inc(pv_done, 1)

            def denominators(p):
                pe.wait_ge(act_round, p * ROUNDS + 2)
                pe.wait_ge(dve_round, p * ROUNDS + 2)
                pe.wait_ge(sum_done, p * TILES + PREV_SLOTS)
                for h in range(2):
                    for n in range(NH):
                        at = (2 * h + n) * DEN_ROWS
                        last = mm(proj[at:at + DEN_ROWS, 0, :], ones[:, 0:DEN_ROWS], sums[:, n, h, :],
                                  start=True, stop=True)
                last.then_inc(den_ready, 1)

            def k_of(buf, t):
                return k_parts[:, buf, :, t * P:(t + 1) * P] if buf < 2 else k_tail[:, :, t * P:(t + 1) * P]

            def chunk(p, T, buf, n, src, stage_wait=None, opening=False):
                pe.wait_ge(act_round, n - 1)
                pe.wait_ge(dve_round, n - 1)
                for t in range(CT):
                    qk(T + t, k_of(buf, t))
                    if opening and t == 0:
                        denominators(p)
                    if t >= LAG:
                        if opening and t == LAG:
                            pe.wait_ge(acc_copied, p + 1)
                        pv(T + (t - LAG), t - LAG, v_sb[:, buf, t - LAG, :], first=(opening and t == LAG))
                    elif not opening:
                        pv(T + t - LAG, CT - LAG + t, v_sb[:, 1 - buf, CT - LAG + t, :])
                    if t == 1:
                        if opening:
                            pe.wait_ge(den_copied, p + 1)
                        if stage_wait is not None:
                            pe.wait_ge(*stage_wait)
                        project_kv(n, src)

            mm(acc[:, 0, 0:1], ident, ones[:, 0:1], start=True, stop=True).then_inc(pv_done, PREV_SLOTS)
            with pe.Fori(0, pairs) as p:
                chunk(p, p * TILES, 0, kv_round(p, 1), keys_t[:, CK:2 * CK], opening=True)
                pairs_done = p * INNER
                with pe.Fori(0, INNER) as i:
                    for b in range(2):
                        chunk(p, p * TILES + i * (2 * CT) + (b + 1) * CT, 1 - b, kv_round(p, i * 2 + b + 2),
                              stage[:, b, :], stage_wait=(stage_in[b], (pairs_done + i) * 16 + 16))
                chunk(p, p * TILES + (WHOLE - 1) * CT, 1, kv_round(p, WHOLE), keys_t[:, WHOLE * CK:PADDED])
                T = p * TILES + WHOLE * CT
                pe.wait_ge(act_round, kv_round(p, WHOLE))
                pe.wait_ge(dve_round, kv_round(p, WHOLE))
                qk(T, k_of(2, 0))
                pv(T - 2, 2, v_sb[:, 1, 2, :])
                qk(T + 1, k_of(2, 1))
                pv(T - 1, 3, v_sb[:, 1, 3, :])
                pe.wait_ge(weights_copied, p + 2)
                project_kv(p * ROUNDS + ROUNDS + 1, keys_t[:, 0:CK])
                qk(T + 2, k_of(2, 2))
                pv(T, 0, v_tail[:, 0, :])
                pe.wait_ge(act_round, p * ROUNDS + ROUNDS + 1)
                pe.wait_ge(dve_round, p * ROUNDS + ROUNDS + 1)
                project_q(0)
                pe.wait_ge(exp_done, T * 2 + (2 * TAIL_TILES + 1))
                project_q(1)
                pv(T + 1, 1, v_tail[:, 1, :])
                pv(T + 2, 2, v_tail[:, 2, :], final=True)
            denominators(pairs)

            pe.wait_ge(heads_done, pairs)
            pe.wait_ge(act_round, pairs * ROUNDS + 3)
            pe.wait_ge(dve_round, pairs * ROUNDS + 3)
            pe.wait_ge(late_in, 48)

            def project_out(tiles_of):
                for j in tiles_of:
                    bias_row(tiles(sc0)[:, j, :], b_x, start=(j % HT == 0))
                    for n in range(pairs - 1):
                        mm(tiles(sc0)[:, j, :], heads_t[:, n, j * P:(j + 1) * P], w_xo[:, n, :],
                           start=False, stop=False)

            def project_last_pair(g):
                pe.wait_ge(heads_done, pairs + g + 1)
                for j in range(g * HT, (g + 1) * HT):
                    last = mm(tiles(sc0)[:, j, :], heads_t[:, pairs - 1, j * P:(j + 1) * P], w_xo[:, pairs - 1, :],
                              start=False, stop=(j % HT == HT - 1))
                last.then_inc(out_ready, 1)

            def turn_x2(g):
                pe.wait_ge(x2_ready, g + 1)
                for j in range(g * HT, (g + 1) * HT):
                    last = turn(sc1[:, j * P:(j + 1) * P], x2[:, j, :], ident)
                last.then_inc(x2_turned, 1)

            def route(g):
                pe.wait_ge(x2_copied, g + 1)
                if g:
                    pe.wait_ge(logits_copied, g)
                for j in range(g * HT, (g + 1) * HT):
                    last = mm(proj[:, 0, j * E:(j + 1) * E], x2_t[:, j * P:(j + 1) * P], w_router[:, :],
                              start=True, stop=True)
                last.then_inc(logits_ready, 1)

            def find_places(g):
                pe.wait_ge(chosen_ready, g + 1)
                if g:
                    pe.wait_ge(moe_added, E + 1)
                half = slice(g * HT * E, (g + 1) * HT * E)
                at = LT * E + g * HT * E
                mm(places[g][:, half], earlier, chosen.rearrange("p j e -> p (j e)")[:, half], start=True, stop=False)
                mm(places[g][:, half], ones[:, :], before[:, 2, at:at + HT * E], start=False, stop=True)\
                    .then_inc(places_ready, 1)

            experts = w_experts[:, :, :].rearrange("d e f -> d (e f)")

            def run_experts(j):
                if j in (0, 2):
                    pe.wait_ge(out_read, j // 2 + 1)
                    pe.wait_ge(x2_copied, j // 2 + 1)
                if j == 3:
                    pe.wait_ge(logits_copied, NH)
                    pe.wait_ge(places_read, 1)
                if j >= 4:
                    pe.wait_ge(moe_added, (j // 2 - 1) * (E + 1))
                if j == 5:
                    pe.wait_ge(places_read, NH)
                for n in range(2):
                    last = mm(expert_banks[j % 4][:, n, :], x2_t[:, j * P:(j + 1) * P],
                              experts[:, n * HALF:(n + 1) * HALF], start=True, stop=True)
                last.then_inc(moe_ready, 1)

            project_out(range(HT))
            project_last_pair(0)
            project_out(range(HT, LT - 1))
            turn_x2(0)
            route(0)
            project_out(range(LT - 1, LT))
            project_last_pair(1)
            run_experts(0)
            find_places(0)
            run_experts(1)
            turn_x2(1)
            route(1)
            run_experts(2)
            run_experts(3)
            find_places(1)
            for j in range(4, LT):
                run_experts(j)

        @block.vector
        def _(dve):
            v = nc.vector
            links = 0

            def link(ins):
                nonlocal links
                links += 1
                ins.then_inc(dve_link, 1)
                dve.wait_ge(dve_link, links)

            v.memset(ones[:, :], 1.0).then_inc(ones_set, 1)

            def key_statistics(g):
                dve.wait_ge(key_in[g], 16)
                for j in range(g * GC, (g + 1) * GC):
                    last = v.bn_stats(key_stat[:, j, :], keys_raw[:, j, :])
                link(last)
                for j in range(g * GC, (g + 1) * GC):
                    last = v.bn_aggr(key_mv[:, j, :], key_stat[:, j, :])
                last.then_inc(key_stats, 1)

            def key_norm(g):
                dve.wait_ge(key_stats, g + 1)
                dve.wait_ge(key_rstds, g + 1)
                for j in range(g * GC, (g + 1) * GC):
                    last = v.tensor_scalar(keys_raw[:, j, :], keys_raw[:, j, :], key_mv[:, j, 0:1],
                                           key_rstd[:, j:j + 1], ALU.subtract, ALU.mult)
                last.then_inc(keys_normed, 1)

            key_statistics(0)
            for g in range(1, ST // GC):
                key_statistics(g)
                if g <= DVE_GROUPS:
                    key_norm(g - 1)
            dve.wait_ge(last_key_in, 16)
            link(v.bn_stats(key_stat[0:SR, ST, :], keys_last[:, :]))
            v.bn_aggr(key_mv[0:SR, ST, :], key_stat[0:SR, ST, :]).then_inc(key_stats, 1)
            def gate_conv(b):
                dve.wait_ge(conv_ready, b + 1)
                v.tensor_tensor(y_t[:, b * BLK:(b + 1) * BLK], u_t[:, b * BLK:(b + 1) * BLK], conv_bank[b],
                                ALU.mult).then_inc(y_done, 1)

            def accumulate(f, d):
                n = NB - d

                def window(t):
                    return t[:, f, d:d + 1, :].broadcast_to([P, n, D])

                second_cos = h_cos_n if f == 0 else h_cos[:, 1, :, :]
                yc, ys = y_cos[:, f, d:NB, :], y_sin[:, f, d:NB, :]
                pc, ps, pcs, psc = (products[:, i, 0:n, :] for i in range(4))
                vc, vs = v_cos[:, f, 0:n, :], v_sin[:, f, 0:n, :]
                v.tensor_tensor(pc if d else yc, vc, window(h_cos), ALU.mult)
                v.tensor_tensor(pcs if d else ys, vc, window(h_sin), ALU.mult)
                v.tensor_tensor(ps, vs, window(h_sin), ALU.mult)
                link(v.tensor_tensor(psc, vs, second_cos[:, d:d + 1, :].broadcast_to([P, n, D]), ALU.mult))
                if d:
                    v.tensor_tensor(yc, yc, pc, ALU.add)
                    link(v.tensor_tensor(ys, ys, pcs, ALU.add))
                v.tensor_tensor(yc, yc, ps, ALU.subtract)
                last = v.tensor_tensor(ys, ys, psc, ALU.add)
                if f == 0:
                    link(last)
                else:
                    last.then_inc(spectrum_done, 1)
                    if d < NB - 1:
                        dve.wait_ge(spectrum_done, d + 1)

            dve.wait_ge(act_step, did("h_sin0"))
            link(v.tensor_copy(h_cos_n, h_cos[:, 0, :, :]))
            link(v.tensor_copy(h_cos_n[0:1, :, :], h_sin[0:1, 0, :, :]))
            link(v.memset(h_sin[0:1, 0, :, :], 0.0))
            for d in range(NB):
                accumulate(0, d)
                if d == 0:
                    dve.wait_ge(key_stats, ST // GC + 1)
                    dve.wait_ge(key_rstds, ST // GC + 1)
                    v.tensor_scalar(keys_last[:, :], keys_last[:, :], key_mv[0:SR, ST, 0:1], key_rstd[0:SR, ST:TILES],
                                    ALU.subtract, ALU.mult).then_inc(keys_normed, 1)
            v.memset(scratch[:, 4:5], 0.0).then_inc(half_spectrum_done, 1)
            dve.wait_ge(act_step, did("h_sin1"))
            for d in range(NB):
                accumulate(1, d)
                if d == NB - 2:
                    gate_conv(0)
                    gate_conv(1)
            gate_conv(2)
            gate_conv(3)

            def row_statistics(norm, g, frm):
                for j in range(g * HT, (g + 1) * HT):
                    last = v.bn_stats(row_stat[:, norm, j, :], frm[:, j, :])
                link(last)
                for j in range(g * HT, (g + 1) * HT):
                    last = v.bn_aggr(row_mv[:, norm, j, :], row_stat[:, norm, j, :])
                last.then_inc(row_stats, 1)

            def row_norm(norm, g, to, frm):
                n = NORMS.index((norm, g)) + 1
                dve.wait_ge(row_stats, n)
                dve.wait_ge(row_rstds, n)
                for j in range(g * HT, (g + 1) * HT):
                    last = v.tensor_scalar(to[:, j, :], frm[:, j, :], row_mv[:, norm, j, 0:1],
                                           row_rstd[:, norm, j:j + 1], ALU.subtract, ALU.mult)
                return last

            def add_rows(g, to, rows):
                half = slice(g * HT, (g + 1) * HT)
                return v.tensor_tensor(to[:, half, :], rows[:, half, :], tiles(sc0)[:, half, :], ALU.add)

            def k_low(n, buf, width):
                dve.wait_ge(act_round, n)
                dst = k_parts[:, buf, :, :] if buf < 2 else k_tail[:, :, :]
                for h in range(2):
                    r, other = slice(h * DH, (h + 1) * DH), slice((1 - h) * DH, (2 - h) * DH)
                    last = v.tensor_tensor(dst[other, h, 0:width], proj[r, 0, 0:width],
                                           dst[r, h, 0:width].bitcast(F32), ALU.subtract)
                last.then_inc(dve_round, 1)

            dve.wait_ge(attn_ready, 1)
            link(add_rows(0, resid, x_sb))
            row_statistics(0, 0, resid)
            dve.wait_ge(attn_ready, 2)
            link(add_rows(1, resid, x_sb))
            row_statistics(0, 1, resid)
            for g in range(NH):
                link(row_norm(0, g, x1, resid))
                row_statistics(1, g, x1)
            row_norm(1, 0, lat, x1).then_inc(lat_ready, 1)
            k_low(1, 0, CK)
            row_norm(1, 1, lat, x1).then_inc(lat_ready, 1)
            for g in range(NH):
                dve.wait_ge(act_round, g + 2)
                for h in range(2):
                    last = v.tensor_tensor(q_parts[:, h, 1, g * HALF:(g + 1) * HALF],
                                           q_bank[h][:, g * HALF:(g + 1) * HALF],
                                           q_parts[:, h, 0, g * HALF:(g + 1) * HALF].bitcast(F32), ALU.subtract)
                last.then_inc(dve_round, 1)
            def q_low(n, h):
                dve.wait_ge(act_round, n)
                v.tensor_tensor(q_parts[:, h, 1, :], q_bank[h], q_parts[:, h, 0, :].bitcast(F32), ALU.subtract)\
                    .then_inc(dve_round, 1)

            def clip(T, slot):
                tile = probs[:, slot, :, :, :]
                dve.wait_ge(exp_done, T * 2 + NH + 2)
                v.tensor_scalar(tile, tile, float(np.exp(CLIP)), float(np.exp(-CLIP)), ALU.min, ALU.max)\
                    .then_inc(clip_done, 1)

            def add_up(T, slot, rows=P, first=None):
                tile = probs[0:rows, slot, :, :, :]
                dve.wait_ge(clip_done, T + 1)
                dve.wait_ge(sum_done, T + PREV_SLOTS)
                if first is not None:
                    dve.wait_ge(den_ready, first + 1)
                    v.tensor_copy(sums[:, :, :, :], tile).then_inc(sum_done, 1)
                else:
                    v.tensor_tensor(sums[0:rows, :, :, :], sums[0:rows, :, :, :], tile, ALU.add)\
                        .then_inc(sum_done, 1)

            def chunk(p, T, n, width=CK, buf=0, opening=False):
                clip(T, 0)
                if not opening:
                    add_up(T - 1, CT - 1)
                clip(T + 1, 1)
                add_up(T, 0, first=p if opening else None)
                k_low(n, buf, width)
                clip(T + 2, 2)
                add_up(T + 1, 1)
                clip(T + 3, 3)
                add_up(T + 2, 2)

            def invert(at):
                v.reciprocal(den[:, bass.ds(at, PIECE)], den[:, bass.ds(at, PIECE)]).then_inc(inverted, 1)

            def divide(p, to):
                dve.wait_ge(acc_copied, p + 1)
                dve.wait_ge(inverses_ready, p + 1)
                v.tensor_tensor(heads_flat[:, bass.ds(to * L, L)], unscaled.rearrange("p n q -> p (n q)"),
                                inverses.rearrange("p n q -> p (n q)"), ALU.mult).then_inc(heads_done, 1)

            with dve.Fori(0, pairs) as p:
                chunk(p, p * TILES, kv_round(p, 1), buf=1, opening=True)
                dve.wait_ge(den_copied, p + 1)
                for n in range(FIRST_PIECES):
                    invert(n * PIECE)
                with dve.Fori(0, INNER) as i:
                    invert(i * PIECE + FIRST_PIECES * PIECE)
                    for b in range(2):
                        chunk(p, p * TILES + i * (2 * CT) + (b + 1) * CT, kv_round(p, i * 2 + b + 2), buf=b)
                chunk(p, p * TILES + (WHOLE - 1) * CT, kv_round(p, WHOLE), TAIL_K, 2)
                divide(p, (p + (PAIRS - 1)) % PAIRS)
                T = p * TILES + WHOLE * CT
                clip(T, 0)
                add_up(T - 1, CT - 1)
                clip(T + 1, 1)
                add_up(T, 0)
                k_low(p * ROUNDS + ROUNDS + 1, 0, CK)
                clip(T + 2, 2)
                add_up(T + 1, 1)
                q_low(p * ROUNDS + ROUNDS + 2, 0)
                q_low(p * ROUNDS + ROUNDS + 3, 1)
                add_up(T + 2, 2, SR)

            dve.wait_ge(den_copied, pairs + 1)
            v.reciprocal(den, den).then_inc(inverted, PIECES)
            dve.wait_ge(acc_copied, pairs + 1)
            for g in range(NH):
                dve.wait_ge(inverses_ready, pairs + g + 1)
                v.tensor_tensor(heads_t[:, PAIRS - 1, g * HALF:(g + 1) * HALF], unscaled[:, g, :],
                                inverses[:, g, :], ALU.mult).then_inc(heads_done, 1)

            def residual(g):
                dve.wait_ge(out_ready, g + 1)
                add_rows(g, moe, x1).then_inc(out_read, 1)
                dve.wait_ge(out_read, g + 1)
                row_statistics(2, g, moe)

            def choose(g):
                half = slice(g * HT, (g + 1) * HT)
                dve.wait_ge(logits_copied, g + 1)
                for j in range(g * HT, (g + 1) * HT):
                    last = v.max(top[:, j, :], logits[:, j, :])
                link(last)
                for j in range(g * HT, (g + 1) * HT):
                    last = v.max_index(top_at[:, j, :], top[:, j, :], logits[:, j, :])
                link(last)
                v.tensor_tensor(weight[:, 0, half], top[:, half, 1], top[:, half, 0], ALU.subtract).then_inc(gap_ready, 1)
                link(v.tensor_copy(top_no[:, half, :], top_at[:, half, :]))
                v.tensor_tensor(gate_one[:, half, :], expert_no[:, half, :],
                                top_no[:, half, 0:1].broadcast_to([P, HT, E]), ALU.is_equal)
                link(v.tensor_tensor(gate_two[:, half, :], expert_no[:, half, :],
                                     top_no[:, half, 1:2].broadcast_to([P, HT, E]), ALU.is_equal))
                link(v.tensor_tensor(chosen[:, half, :], gate_one[:, half, :], gate_two[:, half, :], ALU.add))
                at, frm = LT * E + g * HT * E, chosen_pad
                for i, (near, far) in enumerate(((1, 2), (0, 2), (0, 4))):
                    last = v.tensor_tensor(before[:, i, at:at + HT * E], frm[:, at - near * E:at - near * E + HT * E],
                                           frm[:, at - far * E:at - far * E + HT * E], ALU.add)
                    frm = before[:, i, :]
                    if i < 2:
                        link(last)
                last.then_inc(chosen_ready, 1)

            def make_gates(g):
                half = slice(g * HT, (g + 1) * HT)

                def per_tile(i):
                    return weight[:, i, half].rearrange("p (j o) -> p j o", o=1).broadcast_to([P, HT, E])

                one, two = gate_one[:, half, :], gate_two[:, half, :]
                dve.wait_ge(gap_exp, g + 1)
                link(v.tensor_scalar(weight[:, 2, half], weight[:, 1, half], 1.0, None, ALU.add))
                link(v.reciprocal(weight[:, 2, half], weight[:, 2, half]))
                link(v.tensor_tensor(weight[:, 3, half], weight[:, 1, half], weight[:, 2, half], ALU.mult))
                v.tensor_tensor(one, one, per_tile(2), ALU.mult)
                link(v.tensor_tensor(two, two, per_tile(3), ALU.mult))
                v.tensor_tensor(one, one, two, ALU.add)
                dve.wait_ge(places_ready, g + 1)
                v.tensor_scalar(kept[:, half, :],
                                places[g][:, g * HT * E:(g + 1) * HT * E].rearrange("p (j e) -> p j e", e=E),
                                float(CAP), None, ALU.is_lt).then_inc(places_read, 1)
                dve.wait_ge(places_read, g + 1)
                link(v.tensor_tensor(one, one, kept[:, half, :], ALU.mult))

            def combine(j):
                done = j // 2 * (E + 1)
                dve.wait_ge(moe_ready, j + 2)
                for e in range(E):
                    if e >= 2:
                        dve.wait_ge(moe_added, done + e - 1)
                    for t in range(2):
                        view = expert_banks[(j + t) % 4][:, e // 4, (e % 4) * D:(e % 4 + 1) * D]
                        gate = gate_one[:, j + t, e:e + 1]
                        to = odd[:, (j + t) % 4, :] if e % 2 else x3[:, j + t, :]
                        if e == 1:
                            last = v.tensor_scalar(to, view, gate, None, ALU.mult)
                        else:
                            last = v.scalar_tensor_tensor(out=to, in0=view, scalar=gate,
                                                          in1=to if e else x2[:, j + t, :],
                                                          op0=ALU.mult, op1=ALU.add)
                    last.then_inc(moe_added, 1)
                dve.wait_ge(moe_added, done + E)
                v.tensor_tensor(x3[:, j:j + 2, :], x3[:, j:j + 2, :], odd[:, j % 4:j % 4 + 2, :], ALU.add)\
                    .then_inc(moe_added, 1)

            residual(0)
            v.memset(chosen_pad[:, 0:LT * E], 0.0)
            v.memset(before[:, :, 0:LT * E], 0.0)
            row_norm(2, 0, x2, moe).then_inc(x2_ready, 1)
            choose(0)
            residual(1)
            make_gates(0)
            row_norm(2, 1, x2, moe).then_inc(x2_ready, 1)
            combine(0)
            choose(1)
            combine(2)
            make_gates(1)
            dve.wait_ge(moe_added, 2 * (E + 1))
            row_statistics(3, 0, x3)
            combine(4)
            row_norm(3, 0, moe, x3).then_inc(final_ready, 1)
            combine(6)
            dve.wait_ge(moe_added, 4 * (E + 1))
            row_statistics(3, 1, x3)
            row_norm(3, 1, moe, x3).then_inc(final_ready, 1)


_INS = ["x", "ctx_1024", "L0_xattn_Wq", "L0_xattn_Wkv", "L0_xattn_Wo", "L0_ffn_We"]


def kernel(**inputs):
    from concourse import bacc
    from concourse.bass_utils import run_bass_kernel_spmd

    arrays = {n: np.ascontiguousarray(inputs[n]) for n in _INS}
    arrays["router_t"] = np.ascontiguousarray(np.asarray(inputs["L0_ffn_Wr"]).T)
    arrays.update(constants())

    def pad_rows(t):
        return np.concatenate([t, np.zeros((P - t.shape[0], t.shape[1]), t.dtype)])

    column = [inputs[n] for n in ("L0_attn_bu", "L0_attn_b1", "L0_attn_b2", "L0_xattn_ln_l_w", "L0_xattn_ln_l_b",
                                  "L0_xattn_ln_c_w", "L0_xattn_ln_c_b")]
    columns = np.zeros((P, len(column)), np.float32)
    for i, n in enumerate(column):
        columns[:n.shape[0], i] = n
    arrays["const_pack"] = np.concatenate([arrays.pop("c_pack"), columns], 1)
    arrays["filter_pack"] = pad_rows(np.concatenate([inputs["L0_attn_W1"], inputs["L0_attn_W2"],
                                                     inputs["L0_attn_W3"]], 1))
    arrays["c_pe"] = pad_rows(arrays["c_pe"])
    arrays["conv_pack"] = np.stack([inputs["L0_attn_Wu"], inputs["L0_attn_Wv"], inputs["L0_attn_Wo"]])
    arrays["row_pack"] = np.stack([inputs["L0_attn_bv"], inputs["L0_attn_b3"], inputs["L0_attn_bo"],
                                   inputs["L0_xattn_bo"]])
    nc = bacc.Bacc("TRN2", target_bir_lowering=False, num_devices=1)
    aps = {n: nc.dram_tensor(f"in_{n}", v.shape, mybir.dt.from_np(v.dtype), kind="ExternalInput").ap()
           for n, v in arrays.items()}
    out = nc.dram_tensor("out", (1, L, D), F32, kind="ExternalOutput").ap()
    build(nc, aps, out)
    r = run_bass_kernel_spmd(nc, [{f"in_{n}": v for n, v in arrays.items()}], core_ids=[0])
    return r.results[0]["out"]
```
